# Optimizing a Trainium2 kernel written in Bass

```python
import numpy as np
import jax
import jax.numpy as jnp

def _softmax(x, axis=-1):
    return jax.nn.softmax(x, axis=axis)

def _gelu(x):
    return jax.nn.gelu(x, approximate=True)

def _silu(x):
    return jax.nn.silu(x)

def _sigmoid(x):
    return jax.nn.sigmoid(x)

def _layernorm(x, axis=-1, eps=1e-05):
    m = jnp.mean(x, axis=axis, keepdims=True)
    v = jnp.var(x, axis=axis, keepdims=True)
    return (x - m) / jnp.sqrt(v + eps)

def _scatter_add(tgt, idx, src, axis=0):
    return tgt.at[idx].add(src)

def _segment_sum(src, seg, n):
    return jax.ops.segment_sum(src, seg, n)
kernel_name = 'mk_vit_tower_d1_tok_img1024_r4_361add'

def setup_inputs(seed: int=0):
    np.random.seed(seed)
    _w = jnp.asarray

    def _rec_inputs():
        import jax
        import jax.numpy as jnp
        _rk = jax.random.key(seed)
        x = -7.10856e-05 + 0.999911 * jax.random.normal(jax.random.fold_in(_rk, 1), (16, 1, 1024, 256), jnp.float32)
        return x
    x = _rec_inputs()

    def _L0_tok_setup():
        import jax, jax.numpy as jnp
        import numpy as np
        B, T, X, D, H = (16, 1, 1024, 256, 128)
        key = jax.random.key(seed)
        k0, k1, k2 = jax.random.split(key, 3)
        s1 = 1.0 / np.sqrt(D)
        s2 = 1.0 / np.sqrt(H)
        return {'encoder_outputs': jax.random.normal(k0, (B, T, X, D), dtype=jnp.float32), 'W1': jax.random.uniform(k1, (D, H), minval=-s1, maxval=s1, dtype=jnp.float32), 'b1': jnp.zeros((H,), dtype=jnp.float32), 'W2': jax.random.uniform(k2, (H, 1), minval=-s2, maxval=s2, dtype=jnp.float32), 'b2': jnp.zeros((1,), dtype=jnp.float32)}
    _L0_tok_all = _L0_tok_setup()
    _L0_tok_in = {k: v for k, v in _L0_tok_all.items() if k in ('W1', 'b1', 'W2', 'b2')}
    del _L0_tok_all

    def _L0_attn_setup():
        import jax, jax.numpy as jnp
        import numpy as np
        T, B, D = (512, 8, 256)
        N_STATE, BLK = (256, 8)
        NB = N_STATE // BLK

        def _reference_tuple_inner(x, W_k, W_v, W_q):
            Tn, Bn, Dn = x.shape
            xf = x.reshape(Tn * Bn, Dn)
            k = (xf @ W_k.T).reshape(Tn, Bn, NB, BLK)
            v = (xf @ W_v.T).reshape(Tn, Bn, NB, BLK)
            q = (xf @ W_q.T).reshape(Tn, Bn, NB, BLK)
            S0 = jnp.zeros((Bn, NB, BLK, BLK), dtype=x.dtype)

            def step(S, kvq):
                k_t, v_t, q_t = kvq
                k_norm = k_t / (jnp.linalg.norm(k_t, axis=-1, keepdims=True) + 1e-06)
                retrieved = jnp.einsum('bnij,bnj->bni', S, k_norm)
                delta = v_t - retrieved
                S_new = jnp.tanh(S + jnp.einsum('bni,bnj->bnij', delta, k_norm))
                Sq = jnp.einsum('bnij,bnj->bni', S_new, q_t).reshape(Bn, NB * BLK)
                out = Sq * jax.nn.silu(Sq)
                return (S_new, out)
            S_final, outputs = jax.lax.scan(step, S0, (k, v, q))
            return (outputs, S_final)
        key = jax.random.key(seed)
        k1, k2, k3, k4 = jax.random.split(key, 4)
        scale = float(np.sqrt(2.0 / (N_STATE + D)))
        return {'x': jax.random.normal(k1, (T, B, D), dtype=jnp.float32), 'W_k': jax.random.normal(k2, (N_STATE, D), dtype=jnp.float32) * scale, 'W_v': jax.random.normal(k3, (N_STATE, D), dtype=jnp.float32) * scale, 'W_q': jax.random.normal(k4, (N_STATE, D), dtype=jnp.float32) * scale}
    _L0_attn_all = _L0_attn_setup()
    _L0_attn_in = {k: v for k, v in _L0_attn_all.items() if k in ('W_k', 'W_v', 'W_q')}
    del _L0_attn_all

    def _L0_ffn_setup():
        import jax, jax.numpy as jnp
        import numpy as np
        NUM_GEMMS = 8
        HIDDEN = 256
        INTER = 1024
        key = jax.random.key(seed)
        k_x, k_w1, k_b1, k_w2, k_b2 = jax.random.split(key, 5)
        x = jax.random.normal(k_x, (8, 512, HIDDEN), dtype=jnp.float32)
        s1 = 1.0 / np.sqrt(HIDDEN)
        s2 = 1.0 / np.sqrt(INTER)
        W1 = jax.random.uniform(k_w1, (NUM_GEMMS, INTER, HIDDEN), jnp.float32, -s1, s1)
        b1 = jax.random.uniform(k_b1, (NUM_GEMMS, INTER), jnp.float32, -s1, s1)
        W2 = jax.random.uniform(k_w2, (NUM_GEMMS, HIDDEN, INTER), jnp.float32, -s2, s2)
        b2 = jax.random.uniform(k_b2, (NUM_GEMMS, HIDDEN), jnp.float32, -s2, s2)
        return {'x': x, 'W1': W1, 'b1': b1, 'W2': W2, 'b2': b2}
    _L0_ffn_all = _L0_ffn_setup()
    _L0_ffn_in = {k: v for k, v in _L0_ffn_all.items() if k in ('W1', 'b1', 'W2', 'b2')}
    del _L0_ffn_all
    return {'x': x, 'L0_tok_W1': _L0_tok_in['W1'], 'L0_tok_b1': _L0_tok_in['b1'], 'L0_tok_W2': _L0_tok_in['W2'], 'L0_tok_b2': _L0_tok_in['b2'], 'L0_attn_W_k': _L0_attn_in['W_k'], 'L0_attn_W_v': _L0_attn_in['W_v'], 'L0_attn_W_q': _L0_attn_in['W_q'], 'L0_ffn_W1': _L0_ffn_in['W1'], 'L0_ffn_b1': _L0_ffn_in['b1'], 'L0_ffn_W2': _L0_ffn_in['W2'], 'L0_ffn_b2': _L0_ffn_in['b2']}

def reference(x, L0_tok_W1, L0_tok_b1, L0_tok_W2, L0_tok_b2, L0_attn_W_k, L0_attn_W_v, L0_attn_W_q, L0_ffn_W1, L0_ffn_b1, L0_ffn_W2, L0_ffn_b2):
    import jax
    import jax.numpy as jnp

    def _L0_tok_ref(encoder_outputs, W1, b1, W2, b2):
        import jax, jax.numpy as jnp
        import numpy as np
        B, T, X, D, H = (16, 1, 1024, 256, 128)
        h = jnp.tanh(encoder_outputs @ W1 + b1)
        energy = h @ W2 + b2
        energy = jnp.transpose(energy, (0, 3, 2, 1))
        weights = jax.nn.softmax(jnp.squeeze(energy, -1), axis=1)
        out = (encoder_outputs * weights[..., None]).sum(axis=1)
        return out

    def _L0_attn_ref(x, W_k, W_v, W_q):
        import jax, jax.numpy as jnp
        import numpy as np
        T, B, D = (512, 8, 256)
        N_STATE, BLK = (256, 8)
        NB = N_STATE // BLK

        def _reference_tuple_inner(x, W_k, W_v, W_q):
            Tn, Bn, Dn = x.shape
            xf = x.reshape(Tn * Bn, Dn)
            k = (xf @ W_k.T).reshape(Tn, Bn, NB, BLK)
            v = (xf @ W_v.T).reshape(Tn, Bn, NB, BLK)
            q = (xf @ W_q.T).reshape(Tn, Bn, NB, BLK)
            S0 = jnp.zeros((Bn, NB, BLK, BLK), dtype=x.dtype)

            def step(S, kvq):
                k_t, v_t, q_t = kvq
                k_norm = k_t / (jnp.linalg.norm(k_t, axis=-1, keepdims=True) + 1e-06)
                retrieved = jnp.einsum('bnij,bnj->bni', S, k_norm)
                delta = v_t - retrieved
                S_new = jnp.tanh(S + jnp.einsum('bni,bnj->bnij', delta, k_norm))
                Sq = jnp.einsum('bnij,bnj->bni', S_new, q_t).reshape(Bn, NB * BLK)
                out = Sq * jax.nn.silu(Sq)
                return (S_new, out)
            S_final, outputs = jax.lax.scan(step, S0, (k, v, q))
            return (outputs, S_final)
        return _reference_tuple_inner(x, W_k, W_v, W_q)[0]

    def _L0_ffn_ref(x, W1, b1, W2, b2):
        import jax, jax.numpy as jnp
        import numpy as np
        NUM_GEMMS = 8
        HIDDEN = 256
        INTER = 1024
        orig_shape = x.shape
        token_num = int(np.prod(orig_shape[:-1]))
        m = token_num // NUM_GEMMS
        xg = x.reshape(NUM_GEMMS, m, HIDDEN)
        h1 = jnp.einsum('gmh,goh->gmo', xg, W1) + b1[:, None, :]
        h2 = jnp.einsum('gmo,gho->gmh', h1, W2) + b2[:, None, :]
        return h2.reshape(orig_shape)
    h = _L0_tok_ref(x, L0_tok_W1, L0_tok_b1, L0_tok_W2, L0_tok_b2)
    h = h + _L0_attn_ref(_layernorm(h, axis=-1), L0_attn_W_k, L0_attn_W_v, L0_attn_W_q)
    h = h + _L0_ffn_ref(_layernorm(h, axis=-1), L0_ffn_W1, L0_ffn_b1, L0_ffn_W2, L0_ffn_b2)
    return h

_drawn_inputs = setup_inputs


def setup_inputs(seed=0):
    import zlib

    import numpy as np

    out = dict(_drawn_inputs(seed))
    spreads = {'L0_tok_b1': (0.0, 0.1)}
    factors = {'L0_ffn_b1': 5.905, 'L0_ffn_b2': 6.78}
    for name, (base, spread) in spreads.items():
        noise = np.random.default_rng([zlib.crc32(name.encode()), seed]).standard_normal(out[name].shape)
        drawn = base * np.exp(spread * noise) if base else spread * noise
        out[name] = jnp.asarray(drawn.astype(out[name].dtype))
    for name, factor in factors.items():
        out[name] = (out[name] * factor).astype(out[name].dtype)
    return out
```

```python
import concourse.bass as bass
from concourse import mybir
from contextlib import ExitStack

STEPS, BATCH, DIM = 16, 1024, 256
HIDDEN = 128
BLOCKS, BLK = 32, 8
GROUPS, INTER = 8, 1024
LN_EPS, NORM_EPS = 1e-5, 1e-6

P = 128
KT = DIM // P
SLOTS = STEPS * BATCH // P
LANES = BATCH // P
PER_GROUP = SLOTS // GROUPS
QUAD = 4
PLANE = BLOCKS * BLK
STATE = BLK * PLANE
HALF = STATE // 2
OT = INTER // P

L_XT = 21
L_TOK = 18
L_XW = 12
L_KEY = 7
L_RET = 2
L_DEL = 1
L_UPD = 0
L_QRY = -1
L_OUT = -2
L_FFN = -7
FIRST_TURN, LAST_TURN = -L_XT, SLOTS - 1 - L_FFN
LOOP_FROM = 11
LOOP_TURNS = 16
LOOP_COUNT = (SLOTS - L_XT - LOOP_FROM) // LOOP_TURNS
LOOP_TO = LOOP_FROM + LOOP_COUNT * LOOP_TURNS


def vit_tower_kernel(nc, x_rows, x_cols, tok_w1, tok_b1, tok_w2, tok_b2, w_k, w_q, w_v,
                     ffn_w1, ffn_b1, ffn_w2, ffn_b2, out):
    f32 = mybir.dt.float32
    i32 = mybir.dt.int32
    ALU = mybir.AluOpType
    ACT = mybir.ActivationFunctionType
    AX = mybir.AxisListType

    ctx = ExitStack()
    with ctx:
        def sb(name, shape, dt=f32):
            return ctx.enter_context(nc.sbuf_tensor(name, shape, dt))

        def pb(name, shape):
            return ctx.enter_context(nc.psum_tensor(name, shape, f32))

        def sem(name):
            return ctx.enter_context(nc.semaphore(name))

        state = sb("state", [P, LANES, STATE])
        ret_prod = sb("ret_prod", [P, STATE])
        out_prod = sb("out_prod", [P, STATE])
        xt_in = sb("xt_in", [P, 2, QUAD, KT, P])
        x_in = sb("x_in", [P, 2, QUAD, DIM])
        xw = sb("xw", [P, 16, DIM])
        xn = sb("xn", [P, 2, DIM])
        xnT = sb("xnT", [P, 16, KT, P])
        key = sb("key", [P, 8, DIM])
        key_sq = sb("key_sq", [P, 2, DIM])
        nkey = sb("nkey", [P, 4, DIM])
        deltaT = sb("deltaT", [P, 2, KT, P])
        silu = sb("silu", [P, 2, DIM])
        outT = sb("outT", [P, 2, KT, P])
        h2 = sb("h2", [P, 8, DIM])
        xn2 = sb("xn2", [P, 2, DIM])
        xn2T = sb("xn2T", [P, 2, KT, P])
        y = sb("y", [P, 4, DIM])
        th = sb("th", [P, QUAD, P])
        w1g = sb("w1g", [P, OT, DIM])
        w2g = sb("w2g", [P, OT, DIM])
        b1g = sb("b1g", [P, OT])
        b2g = sb("b2g", [P, KT])
        wc = sb("wc", [P, KT, DIM])
        bc = sb("bc", [P, KT, P])
        wk_s = sb("wk_s", [P, KT, DIM])
        wq_s = sb("wq_s", [P, KT, DIM])
        wv_s = sb("wv_s", [P, KT, DIM])
        tw1 = sb("tw1", [P, KT, HIDDEN])
        tb1 = sb("tb1", [P, 1])
        tw2 = sb("tw2", [P, 1])
        tb2 = sb("tb2", [P, 1])
        ident = sb("ident", [P, P])
        eul = sb("eul", [P, QUAD])
        mone = sb("mone", [P, QUAD])
        mhalf = sb("mhalf", [P, QUAD])
        energy = sb("energy", [P, QUAD])
        sm = sb("sm", [P, 3, QUAD])
        weight = sb("weight", [P, 2, QUAD])
        raw1 = sb("raw1", [P, 2, 6])
        raw2 = sb("raw2", [P, 2, 6])
        stat1 = sb("stat1", [P, 2, QUAD, 2])
        stat2 = sb("stat2", [P, 2, QUAD, 2])
        ve1 = sb("ve1", [P, QUAD])
        ve2 = sb("ve2", [P, QUAD])
        mr1 = sb("mr1", [P, QUAD])
        mr2 = sb("mr2", [P, QUAD])
        rstd1 = sb("rstd1", [P, 2, QUAD])
        rstd2 = sb("rstd2", [P, 2, QUAD])
        shift1 = sb("shift1", [P, 2, QUAD])
        shift2 = sb("shift2", [P, 2, QUAD])
        QB = QUAD * BLOCKS
        sumsq = sb("sumsq", [P, 2, QB])
        seed_i = sb("seed_i", [P, QB], i32)
        root = sb("root", [P, 3, QB])
        nt = sb("nt", [P, 6, QB])
        nnorm = sb("nnorm", [P, QB])
        nrecip = sb("nrecip", [P, 2, QB])
        warm = sb("warm", [P, 1])

        upd = pb("upd", [P, STATE])
        del_b = pb("del_b", [P, 512])
        qry_b = pb("qry_b", [P, 512])
        rec_b = pb("rec_b", [P, 512])
        frt_b = pb("frt_b", [P, 512])

        setup_in = sem("setup_in")
        ident_ok = sem("ident_ok")
        state_zero = sem("state_zero")
        warm_ok = sem("warm_ok")
        xt_loaded = [sem("xt_loaded0"), sem("xt_loaded1")]
        x_loaded = [sem("x_loaded0"), sem("x_loaded1")]
        group_in = sem("group_in")
        stored = [sem(f"stored{i}") for i in range(4)]
        tok_ready = sem("tok_ready")
        th_ready = sem("th_ready")
        en_ready = sem("en_ready")
        e_ready = sem("e_ready")
        sm_step = sem("sm_step")
        xw_ready = sem("xw_ready")
        raw1_ok = sem("raw1_ok")
        stat1_ok = sem("stat1_ok")
        ln1_step = sem("ln1_step")
        xn_ready = sem("xn_ready")
        tr_ready = sem("tr_ready")
        xnT_ready = sem("xnT_ready")
        xn2T_ready = sem("xn2T_ready")
        key_b_ready = sem("key_b_ready")
        key_ready = sem("key_ready")
        ksq_ready = sem("ksq_ready")
        sumsq_ok = sem("sumsq_ok")
        seed_sh = sem("seed_sh")
        seed_ok = sem("seed_ok")
        newt = sem("newt")
        NEWT = 12
        nrec_ok = sem("nrec_ok")
        nkey_ok = sem("nkey_ok")
        ret_done = sem("ret_done")
        dT_ready = sem("dT_ready")
        dT_out = sem("dT_out")
        del_ready = sem("del_ready")
        outer_done = sem("outer_done")
        sum_done = sem("sum_done")
        state_new = sem("state_new")
        qry_ready = sem("qry_ready")
        outp_done = sem("outp_done")
        sqT_ready = sem("sqT_ready")
        silu_ready = sem("silu_ready")
        outT_ready = sem("outT_ready")
        ik_ready = sem("ik_ready")
        h2_ready = sem("h2_ready")
        raw2_ok = sem("raw2_ok")
        stat2_ok = sem("stat2_ok")
        ln2_step = sem("ln2_step")
        xn2_ready = sem("xn2_ready")
        y_ready = sem("y_ready")
        wc_b_ready = sem("wc_b_ready")
        wc_ready = sem("wc_ready")
        bc_b_ready = sem("bc_b_ready")
        bc_ready = sem("bc_ready")

        gp_past = sem("gp_past")
        dve_past = sem("dve_past")

        block = ctx.enter_context(nc.Block())

        SETUP_DMAS = 8

        class Turn:

            def __init__(self, it, n):
                self.it, self.n, self.static = it, n, isinstance(it, int)

            def has(self, lead):
                return not self.static or 0 <= self.n + lead < SLOTS

            def slot(self, lead):
                return self.n + lead

            def wait(self, eng, s, lead, per=1, part=None):
                c = per * (self.n + lead) + (per if part is None else part)
                if self.static:
                    c = min(c, per * SLOTS)
                self._wait(eng, s, per * 16, c)

            def quad(self, lead):
                n = self.n + lead
                return n // QUAD if n % QUAD == 0 and self.has(lead) else None

            def wait_quad(self, eng, s, q, per, part):
                c = per * q + part
                self._wait(eng, s, per * 4, c)

            def _wait(self, eng, s, per_turn, c):
                assert self.static or c > 0
                if c > 0 or not self.static:
                    eng.wait_ge(s, per_turn * self.it + c)

        def run(eng, turn):
            for n in range(FIRST_TURN, LOOP_FROM):
                turn(Turn(0, n))
            with eng.Fori(0, LOOP_COUNT) as it:
                for n in range(LOOP_FROM, LOOP_FROM + LOOP_TURNS):
                    turn(Turn(it, n))
            for n in range(LOOP_TO, LAST_TURN + 1):
                turn(Turn(0, n))

        def planes(ap):
            return ap.rearrange("p (j n i) -> p j n i", n=BLOCKS, i=BLK)

        @block.sync
        def _(sp):
            sp.dma_start(tw1[:], tok_w1).then_inc(setup_in, 16)
            sp.dma_start(tb1[:], tok_b1).then_inc(setup_in, 16)
            sp.dma_start(tw2[:], tok_w2).then_inc(setup_in, 16)
            sp.dma_start(tb2[:], tok_b2.broadcast_to([P, 1])).then_inc(setup_in, 16)

            def load_group(g):
                sp.dma_start(w1g[:], ffn_w1[g]).then_inc(group_in, 16)
                sp.dma_start(w2g[:], ffn_w2[g]).then_inc(group_in, 16)
                sp.dma_start(b1g[:], ffn_b1[g]).then_inc(group_in, 16)
                sp.dma_start(b2g[:], ffn_b2[g]).then_inc(group_in, 16)

            def turn(t):
                q = t.quad(L_XT)
                if q is not None:
                    t.wait(sp, tok_ready, L_XT - QUAD - 1)
                    sp.dma_start(xt_in[:, q % 2], x_cols[4 * t.it + q]).then_inc(xt_loaded[q % 2], 16)
                if t.n == FIRST_TURN:
                    sp.dma_start(wk_s[:], w_k).then_inc(setup_in, 16)
                    sp.dma_start(wq_s[:], w_q).then_inc(setup_in, 16)
                    sp.dma_start(wv_s[:], w_v).then_inc(setup_in, 16)
                    load_group(0)
                q = t.quad(L_XW + QUAD)
                if q is not None:
                    t.wait(sp, xw_ready, L_XW - 1)
                    sp.dma_start(x_in[:, q % 2], x_rows[4 * t.it + q]).then_inc(x_loaded[q % 2], 16)
                if (t.n - 8) % 16 == 0 and t.has(L_FFN + PER_GROUP - 1):
                    g = (t.n - 8) // 16 + 1
                    if not t.static or 1 <= g < GROUPS:
                        sp.wait_ge(bc_ready, 2 * t.it + 2 * g)
                        load_group(t.it + g)
                if t.has(L_FFN):
                    s = t.slot(L_FFN)
                    t.wait(sp, y_ready, L_FFN)
                    sp.dma_start(out[16 * t.it + s], y[:, s % 4]).then_inc(stored[s % 4], 16)

            run(sp, turn)
            for i in range(4):
                sp.wait_ge(stored[i], 16 * SLOTS // 4)

        @block.gpsimd
        def _(gp):
            nc.gpsimd.memset(ident[:], 0.0).then_inc(ident_ok, 1)
            gp.wait_ge(ident_ok, 1)
            nc.gpsimd.affine_select(out=ident[:], in_=ident[:], compare_op=ALU.not_equal, fill=1.0, base=0,
                                    pattern=[[-1, P]], channel_multiplier=1).then_inc(ident_ok, 1)
            nc.gpsimd.memset(eul[:], 2.718281828459045).then_inc(ident_ok, 1)
            nc.gpsimd.memset(mone[:], -1.0).then_inc(ident_ok, 1)
            nc.gpsimd.memset(mhalf[:], -0.5).then_inc(ident_ok, 1)
            for b in range(LANES):
                nc.gpsimd.memset(state[:, b], 0.0).then_inc(state_zero, 1)
            gp.wait_ge(ident_ok, 5)
            gp.wait_ge(state_zero, LANES)

            def rstd(t, q, stat, ve, mr, r, sh, steps, stat_ok, used, lead):
                t.wait(gp, stat_ok, lead + QUAD - 1)
                t.wait(gp, used, lead - QUAD - 1)
                b = q % 2
                gp.sem_inc(gp_past, 1)
                nc.gpsimd.tensor_scalar(ve[:], stat[:, b, :, 1], 1.0, LN_EPS, ALU.mult, ALU.add).then_inc(steps, 1)
                t.wait_quad(gp, steps, q, 4, 1)
                nc.gpsimd.tensor_tensor(r[:, b], ve[:], mhalf[:], ALU.pow).then_inc(steps, 1)
                t.wait_quad(gp, steps, q, 4, 2)
                nc.gpsimd.tensor_tensor(mr[:], stat[:, b, :, 0], r[:, b], ALU.mult).then_inc(steps, 1)
                t.wait_quad(gp, steps, q, 4, 3)
                gp.sem_inc(gp_past, 1)
                nc.gpsimd.tensor_scalar(sh[:, b], mr[:], -1.0, 0.0, ALU.mult, ALU.add).then_inc(steps, 1)

            def softmax(t, q):
                t.wait_quad(gp, e_ready, q, 1, 1)
                t.wait(gp, xw_ready, L_XW + 1 - QUAD - 1)
                b = q % 2
                nc.gpsimd.tensor_tensor(sm[:, 0], energy[:], energy[:], ALU.subtract).then_inc(sm_step, 1)
                t.wait_quad(gp, sm_step, q, 4, 1)
                nc.gpsimd.tensor_tensor(sm[:, 1], eul[:], sm[:, 0], ALU.pow).then_inc(sm_step, 1)
                t.wait_quad(gp, sm_step, q, 4, 2)
                nc.gpsimd.tensor_tensor(sm[:, 2], sm[:, 1], mone[:], ALU.pow).then_inc(sm_step, 1)
                t.wait_quad(gp, sm_step, q, 4, 3)
                nc.gpsimd.tensor_tensor(weight[:, b], sm[:, 1], sm[:, 2], ALU.mult).then_inc(sm_step, 1)

            def key_norm(t, q):
                b = q % 2
                s = sumsq[:, b]
                k = [0]

                tt, ts = nc.gpsimd.tensor_tensor, nc.gpsimd.tensor_scalar

                def step(op, dst, *args):
                    if op is ts:
                        gp.sem_inc(gp_past, 1)
                    op(dst, *args).then_inc(newt, 1)
                    k[0] += 1
                    if k[0] < NEWT:
                        t.wait_quad(gp, newt, q, NEWT, k[0])

                t.wait_quad(gp, seed_ok, q, 1, 1)
                step(tt, nt[:, 0], root[:, 0], root[:, 0], ALU.mult)
                step(tt, nt[:, 1], nt[:, 0], s, ALU.mult)
                step(ts, nt[:, 2], nt[:, 1], 0.375, -1.25, ALU.mult, ALU.add)
                step(tt, nt[:, 3], nt[:, 2], nt[:, 1], ALU.mult)
                step(ts, nt[:, 2], nt[:, 3], 1.0, 1.875, ALU.mult, ALU.add)
                step(tt, root[:, 1], root[:, 0], nt[:, 2], ALU.mult)
                step(tt, nt[:, 0], root[:, 1], root[:, 1], ALU.mult)
                step(tt, nt[:, 1], nt[:, 0], s, ALU.mult)
                step(ts, nt[:, 2], nt[:, 1], -0.5, 1.5, ALU.mult, ALU.add)
                step(tt, root[:, 2], root[:, 1], nt[:, 2], ALU.mult)
                step(tt, nt[:, 4], root[:, 2], s, ALU.mult)
                t.wait_quad(gp, nrec_ok, q - 1, 1, 1)
                step(ts, nnorm[:], nt[:, 4], -1.0, -NORM_EPS, ALU.mult, ALU.add)
                assert k[0] == NEWT

            def turn(t):
                q = t.quad(L_KEY - 4)
                if q is not None:
                    key_norm(t, q)
                q = t.quad(L_XW + 1)
                if q is not None:
                    softmax(t, q)
                q = t.quad(L_KEY + 1)
                if q is not None:
                    rstd(t, q, stat1, ve1, mr1, rstd1, shift1, ln1_step, stat1_ok, xn_ready, L_KEY + 1)
                q = t.quad(L_FFN + 1)
                if q is not None:
                    rstd(t, q, stat2, ve2, mr2, rstd2, shift2, ln2_step, stat2_ok, xn2_ready, L_FFN + 1)
                if t.has(L_RET):
                    m = t.slot(L_RET)
                    q = m // QUAD
                    t.wait_quad(gp, nrec_ok, q, 1, 1)
                    t.wait(gp, key_ready, L_RET)
                    t.wait(gp, outer_done, L_RET - 4, per=2)
                    nc.gpsimd.tensor_tensor(
                        nkey[:, m % 4].rearrange("p (j n) -> p j n", n=BLOCKS),
                        key[:, m % 8].rearrange("p (j n) -> p j n", n=BLOCKS),
                        nrecip[:, q % 2, (m % QUAD) * BLOCKS:(m % QUAD + 1) * BLOCKS].unsqueeze(1)
                        .broadcast_to([P, BLK, BLOCKS]), ALU.mult).then_inc(nkey_ok, 1)
                    t.wait(gp, nkey_ok, L_RET)
                    t.wait(gp, dT_ready, L_RET - 1)
                    for half in range(2):
                        t.wait(gp, state_new, L_RET - LANES, per=2, part=half + 1)
                        lo = half * HALF
                        nk = nkey[:, m % 4, half * P:(half + 1) * P]
                        nc.gpsimd.tensor_tensor(
                            ret_prod[:, lo:lo + HALF].rearrange("p (c i) -> p c i", i=BLK),
                            state[:, m % LANES, lo:lo + HALF].rearrange("p (c i) -> p c i", i=BLK),
                            nk.unsqueeze(2).broadcast_to([P, P, BLK]), ALU.mult).then_inc(ret_done, 1)

            run(gp, turn)

        @block.tensor
        def _(pe):
            mm = nc.tensor.matmul

            def tr(dst, src, start=False, stop=False):
                return mm(dst, src, ident[:], start=start, stop=stop, is_transpose=True, skip_group_check=True)

            def plane_sums(prod, dst, done, t, lead, start):
                for j in range(BLK):
                    if j % (BLK // 2) == 0:
                        t.wait(pe, done, lead, per=2, part=j // (BLK // 2) + 1)
                    for h in range(KT):
                        col = j * PLANE + h * P
                        last = tr(dst[:, h * P:(h + 1) * P], prod[:, col:col + P],
                                  start=start and j == 0 and h == 0, stop=(j == BLK - 1))
                return last

            def turn(t):
                new_group = t.slot(L_FFN) % PER_GROUP == 0 and t.has(L_FFN)
                g = t.slot(L_FFN) // PER_GROUP
                if new_group:
                    pe.wait_ge(group_in, 64 * t.it + 64 * (g + 1))
                    t.wait(pe, th_ready, L_TOK - 1)
                    t.wait(pe, ksq_ready, L_KEY - 1)
                    t.wait(pe, xn2T_ready, L_FFN - 1)
                    for k in range(KT):
                        for o in range(OT):
                            last = mm(frt_b[:, k * DIM:(k + 1) * DIM], w1g[:, o, k * P:(k + 1) * P], w2g[:, o, :],
                                      start=(k == 0 and o == 0), stop=(o == OT - 1), skip_group_check=True)
                    last.then_inc(wc_b_ready, 1)
                if t.has(L_QRY):
                    s = t.slot(L_QRY)
                    t.wait(pe, outp_done, L_QRY - 1, per=2)
                    for k in range(KT):
                        last = mm(qry_b[:, 0:DIM], xnT[:, s % 16, k, :], wq_s[:, k, :], start=(k == 0),
                                  stop=(k == KT - 1))
                    last.then_inc(qry_ready, 1)
                if t.has(L_DEL):
                    s = t.slot(L_DEL)
                    t.wait(pe, h2_ready, L_OUT - 1)
                    t.wait(pe, y_ready, L_FFN - 1)
                    for h in range(KT):
                        for k in range(KT):
                            mm(rec_b[:, h * P:(h + 1) * P], wv_s[:, k, h * P:(h + 1) * P], xnT[:, s % 16, k, :],
                               start=(h == 0 and k == 0), stop=False, skip_group_check=True)
                    plane_sums(ret_prod, rec_b, ret_done, t, L_DEL, start=False).then_inc(dT_ready, 1)
                if new_group:
                    pe.wait_ge(wc_ready, t.it + g + 1)
                    for h in range(KT):
                        for o in range(OT):
                            last = mm(frt_b[:, h:h + 1], w2g[:, o, h * P:(h + 1) * P], b1g[:, o:o + 1],
                                      start=(h == 0 and o == 0), stop=(o == OT - 1), skip_group_check=True)
                    last.then_inc(bc_b_ready, 1)
                q = t.n + L_TOK - QUAD
                quad_over = q % QUAD == 0 and t.has(L_TOK - QUAD)
                if quad_over or t.has(L_TOK):
                    if t.n == -L_TOK:
                        pe.wait_ge(setup_in, 16 * 7)
                        pe.wait_ge(ident_ok, 2)
                    t.wait(pe, th_ready, L_TOK - 1)
                    t.wait(pe, ksq_ready, L_KEY - 1)
                    t.wait(pe, xn2T_ready, L_FFN - 1)
                    if new_group:
                        pe.wait_ge(bc_ready, 2 * t.it + 2 * (g + 1))
                opened = False
                if quad_over:
                    for i in range(QUAD):
                        last = mm(frt_b[:, P + i:P + i + 1], th[:, i, :], tw2[:], start=(i == 0), stop=True,
                                  skip_group_check=True)
                        opened = True
                    last.then_inc(en_ready, 1)
                if t.has(L_TOK):
                    s = t.slot(L_TOK)
                    if s % QUAD == 0:
                        pe.wait_ge(xt_loaded[s // QUAD % 2], 32 * t.it + 16 * (s // QUAD // 2 + 1))
                    for k in range(KT):
                        last = mm(frt_b[:, 0:P], tw1[:, k, :], xt_in[:, s // QUAD % 2, s % QUAD, k, :],
                                  start=(k == 0 and not opened), stop=(k == KT - 1), skip_group_check=True)
                    last.then_inc(tok_ready, 1)
                if t.has(L_OUT):
                    t.wait(pe, dT_out, L_DEL)
                    t.wait(pe, h2_ready, L_OUT - 1)
                    t.wait(pe, y_ready, L_FFN - 1)
                    plane_sums(out_prod, rec_b, outp_done, t, L_OUT, start=True).then_inc(sqT_ready, 1)
                if t.has(L_DEL):
                    s = t.slot(L_DEL)
                    t.wait(pe, dT_out, L_DEL)
                    t.wait(pe, outer_done, L_DEL - 1, per=2)
                    for h in range(KT):
                        last = tr(del_b[:, h * P:(h + 1) * P], deltaT[:, s % 2, h, :], start=(h == 0), stop=True)
                    last.then_inc(del_ready, 1)
                if t.has(L_KEY) or t.has(L_FFN):
                    t.wait(pe, th_ready, L_TOK)
                    t.wait(pe, ksq_ready, L_KEY - 1)
                    t.wait(pe, xn2T_ready, L_FFN - 1)
                    if new_group:
                        pe.wait_ge(bc_ready, 2 * t.it + 2 * (g + 1))
                    if quad_over:
                        pe.wait_ge(e_ready, 4 * t.it + q // QUAD + 1)
                    if t.has(L_KEY):
                        s = t.slot(L_KEY)
                        t.wait(pe, xn_ready, L_KEY)
                        for k in range(KT):
                            last = tr(frt_b[:, k * P:(k + 1) * P], xn[:, s % 2, k * P:(k + 1) * P],
                                      start=(k == 0), stop=True)
                    if t.has(L_FFN):
                        s = t.slot(L_FFN)
                        t.wait(pe, xn2_ready, L_FFN)
                        for k in range(KT):
                            last = tr(frt_b[:, DIM + k * P:DIM + (k + 1) * P], xn2[:, s % 2, k * P:(k + 1) * P],
                                      start=(k == 0 and not t.has(L_KEY)), stop=True)
                    last.then_inc(tr_ready, 1)
                if t.has(L_KEY):
                    s = t.slot(L_KEY)
                    t.wait(pe, xnT_ready, L_KEY)
                    if t.has(L_FFN):
                        t.wait(pe, xn2T_ready, L_FFN)
                    for k in range(KT):
                        last = mm(frt_b[:, 0:DIM], xnT[:, s % 16, k, :], wk_s[:, k, :], start=(k == 0),
                                  stop=(k == KT - 1))
                    last.then_inc(key_b_ready, 1)
                if t.has(L_OUT) or t.has(L_FFN):
                    if t.has(L_OUT):
                        s = t.slot(L_OUT)
                        t.wait(pe, outT_ready, L_OUT)
                        for h in range(KT):
                            last = tr(rec_b[:, h * P:(h + 1) * P], outT[:, s % 2, h, :], start=(h == 0), stop=True)
                    if t.has(L_FFN):
                        s = t.slot(L_FFN)
                        if not t.has(L_OUT):
                            t.wait(pe, y_ready, L_FFN - 1)
                            t.wait(pe, h2_ready, L_OUT - 1)
                        t.wait(pe, xn2T_ready, L_FFN)
                        if new_group:
                            pe.wait_ge(bc_ready, 2 * t.it + 2 * (g + 1))
                        for k in range(KT):
                            mm(rec_b[:, DIM:2 * DIM], xn2T[:, s % 2, k, :], wc[:, k, :],
                               start=(k == 0 and not t.has(L_OUT)), stop=False, skip_group_check=True)
                        for h in range(KT):
                            last = tr(rec_b[:, DIM + h * P:DIM + (h + 1) * P], bc[:, h, :], stop=True)
                    last.then_inc(ik_ready, 1)

            run(pe, turn)

        @block.scalar
        def _(act):
            fn = nc.scalar.activation
            act.wait_ge(ident_ok, 2)
            fn(warm[:], ident[:, 0:1], ACT.Silu).then_inc(warm_ok, 1)

            def turn(t):
                if t.has(L_XW):
                    s = t.slot(L_XW)
                    qp = s // QUAD % 2
                    if s % QUAD == 0:
                        act.wait_ge(x_loaded[qp], 32 * t.it + 16 * (s // QUAD // 2 + 1))
                        t.wait_quad(act, sm_step, s // QUAD, 4, 4)
                    t.wait(act, h2_ready, L_XW - 16)
                    t.wait(act, stat1_ok, L_XW - 16)
                    fn(xw[:, s % 16], x_in[:, qp, s % QUAD], ACT.Copy,
                       scale=weight[:, qp, s % QUAD:s % QUAD + 1]).then_inc(xw_ready, 1)
                if t.has(L_KEY):
                    s = t.slot(L_KEY)
                    qp = s // QUAD % 2
                    t.wait_quad(act, ln1_step, s // QUAD, 4, 4)
                    fn(xn[:, s % 2], xw[:, s % 16], ACT.Identity, scale=rstd1[:, qp, s % QUAD:s % QUAD + 1],
                       bias=shift1[:, qp, s % QUAD:s % QUAD + 1]).then_inc(xn_ready, 1)
                if t.has(L_FFN):
                    s = t.slot(L_FFN)
                    qp = s // QUAD % 2
                    t.wait_quad(act, ln2_step, s // QUAD, 4, 4)
                    fn(xn2[:, s % 2], h2[:, s % 8], ACT.Identity, scale=rstd2[:, qp, s % QUAD:s % QUAD + 1],
                       bias=shift2[:, qp, s % QUAD:s % QUAD + 1]).then_inc(xn2_ready, 1)
                new_group = t.slot(L_FFN) % PER_GROUP == 0 and t.has(L_FFN)
                g = t.slot(L_FFN) // PER_GROUP
                if new_group:
                    act.wait_ge(wc_b_ready, t.it + g + 1)
                    fn(wc[:].rearrange("p k d -> p (k d)"), frt_b[:], ACT.Copy).then_inc(wc_ready, 1)
                if t.has(L_DEL):
                    s = t.slot(L_DEL)
                    t.wait(act, dT_ready, L_DEL)
                    t.wait(act, del_ready, L_DEL - 2)
                    fn(deltaT[:, s % 2].rearrange("p h b -> p (h b)"), rec_b[:, 0:DIM], ACT.Copy).then_inc(dT_out, 1)
                if new_group:
                    act.wait_ge(bc_b_ready, t.it + g + 1)
                    for h in range(KT):
                        fn(bc[:, h, :], frt_b[:, h:h + 1].broadcast_to([P, P]), ACT.Identity,
                           bias=b2g[:, h:h + 1]).then_inc(bc_ready, 1)
                q = t.n + L_TOK - QUAD
                if q % QUAD == 0 and t.has(L_TOK - QUAD):
                    if t.n + L_TOK == QUAD:
                        act.wait_ge(setup_in, 16 * 7)
                    act.wait_ge(en_ready, 4 * t.it + q // QUAD + 1)
                    t.wait_quad(act, sm_step, q // QUAD - 1, 4, 4)
                    if t.has(L_TOK):
                        t.wait(act, tok_ready, L_TOK)
                    fn(energy[:], frt_b[:, P:P + QUAD], ACT.Identity, bias=tb2[:]).then_inc(e_ready, 1)
                if t.has(L_TOK):
                    s = t.slot(L_TOK)
                    if t.n + L_TOK == 0:
                        act.wait_ge(setup_in, 16 * 7)
                    t.wait(act, tok_ready, L_TOK)
                    fn(th[:, s % QUAD], frt_b[:, 0:P], ACT.Tanh, bias=tb1[:]).then_inc(th_ready, 1)
                if t.has(L_OUT):
                    s = t.slot(L_OUT)
                    t.wait(act, sqT_ready, L_OUT)
                    fn(silu[:, s % 2], rec_b[:, 0:DIM], ACT.Silu).then_inc(silu_ready, 1)
                if t.has(L_KEY) or t.has(L_FFN):
                    act.wait_ge(tr_ready, 16 * t.it + t.n + L_KEY + 1)
                    if t.has(L_KEY):
                        s = t.slot(L_KEY)
                        t.wait(act, qry_ready, L_KEY - 16)
                        fn(xnT[:, s % 16].rearrange("p k b -> p (k b)"), frt_b[:, 0:DIM],
                           ACT.Copy).then_inc(xnT_ready, 1)
                    if t.has(L_FFN):
                        s = t.slot(L_FFN)
                        fn(xn2T[:, s % 2].rearrange("p k b -> p (k b)"), frt_b[:, DIM:2 * DIM],
                           ACT.Copy).then_inc(xn2T_ready, 1)
                for half in range(2):
                    if t.has(L_UPD):
                        s = t.slot(L_UPD)
                        lo = half * HALF
                        t.wait(act, sum_done, L_UPD, per=2, part=half + 1)
                        if half == 0:
                            t.wait(act, sqT_ready, L_UPD - LANES)
                        fn(state[:, s % LANES, lo:lo + HALF], upd[:, lo:lo + HALF], ACT.Tanh).then_inc(state_new, 1)
                if t.has(L_KEY):
                    s = t.slot(L_KEY)
                    t.wait(act, key_b_ready, L_KEY)
                    t.wait(act, nkey_ok, L_KEY - 8)
                    fn(key[:, s % 8], frt_b[:, 0:DIM], ACT.Copy).then_inc(key_ready, 1)
                    t.wait(act, sumsq_ok, L_KEY - 2)
                    fn(key_sq[:, s % 2], frt_b[:, 0:DIM], ACT.Square).then_inc(ksq_ready, 1)

            run(act, turn)

        @block.vector
        def _(dve):
            tt = nc.vector.tensor_tensor

            def turn(t):
                q = t.quad(L_KEY - 4)
                if q is not None:
                    b = q % 2
                    t.wait(dve, sumsq_ok, L_KEY - 4 + QUAD - 1)
                    t.wait_quad(dve, newt, q - 1, NEWT, NEWT)
                    nc.vector.tensor_scalar(seed_i[:], sumsq[:, b].bitcast(i32), 1, None,
                                            ALU.logical_shift_right).then_inc(seed_sh, 1)
                    t.wait_quad(dve, seed_sh, q, 1, 1)
                    nc.vector.tensor_scalar(root[:, 0].bitcast(i32), seed_i[:], -1.0, float(0x5f3759df),
                                            ALU.mult, ALU.add).then_inc(seed_ok, 1)
                if t.has(L_UPD):
                    s = t.slot(L_UPD)
                    t.wait(dve, nkey_ok, L_UPD)
                    t.wait(dve, del_ready, L_UPD)
                    nk = nkey[:, s % 4].rearrange("p (j n) -> p j n", n=BLOCKS)
                    delta = del_b[:, 0:DIM].rearrange("p (n i) -> p n i", i=BLK)
                    JH = BLK // 2
                    for half in range(2):
                        t.wait(dve, state_new, L_UPD - 1, per=2, part=half + 1)
                        tt(planes(upd[:, half * HALF:(half + 1) * HALF]),
                           delta.unsqueeze(1).broadcast_to([P, JH, BLOCKS, BLK]),
                           nk[:, half * JH:(half + 1) * JH].unsqueeze(3).broadcast_to([P, JH, BLOCKS, BLK]),
                           ALU.mult).then_inc(outer_done, 1)
                    for half in range(2):
                        lo = half * HALF
                        t.wait(dve, outer_done, L_UPD, per=2, part=half + 1)
                        tt(upd[:, lo:lo + HALF], state[:, s % LANES, lo:lo + HALF], upd[:, lo:lo + HALF],
                           ALU.subtract).then_inc(sum_done, 1)
                if t.has(L_OUT):
                    s = t.slot(L_OUT)
                    t.wait(dve, silu_ready, L_OUT)
                    tt(outT[:, s % 2].rearrange("p h b -> p (h b)"), rec_b[:, 0:DIM], silu[:, s % 2],
                       ALU.mult).then_inc(outT_ready, 1)
                if t.has(L_XW):
                    s = t.slot(L_XW)
                    t.wait(dve, xw_ready, L_XW)
                    nc.vector.bn_stats(raw1[:, s % 2], xw[:, s % 16]).then_inc(raw1_ok, 1)
                if t.has(L_QRY):
                    s = t.slot(L_QRY)
                    t.wait(dve, qry_ready, L_QRY)
                    t.wait(dve, sqT_ready, L_QRY - 1)
                    for half in range(2):
                        lo = half * HALF
                        t.wait(dve, state_new, L_QRY, per=2, part=half + 1)
                        tt(out_prod[:, lo:lo + HALF].rearrange("p (c i) -> p c i", i=BLK),
                           state[:, s % LANES, lo:lo + HALF].rearrange("p (c i) -> p c i", i=BLK),
                           qry_b[:, half * P:(half + 1) * P].unsqueeze(2).broadcast_to([P, P, BLK]),
                           ALU.mult).then_inc(outp_done, 1)
                if t.has(L_XW):
                    s = t.slot(L_XW)
                    t.wait(dve, raw1_ok, L_XW)
                    t.wait_quad(dve, ln1_step, s // QUAD - 2, 4, 4)
                    dve.sem_inc(dve_past, 1)
                    nc.vector.bn_aggr(stat1[:, s // QUAD % 2, s % QUAD], raw1[:, s % 2]).then_inc(stat1_ok, 1)
                if t.has(L_OUT) or t.has(L_FFN):
                    dve.wait_ge(ik_ready, 16 * t.it + t.n + L_OUT + 1)
                if t.has(L_OUT):
                    s = t.slot(L_OUT)
                    t.wait(dve, xn2_ready, L_OUT - 8)
                    tt(h2[:, s % 8], rec_b[:, 0:DIM], xw[:, s % 16], ALU.add).then_inc(h2_ready, 1)
                if t.has(L_FFN):
                    s = t.slot(L_FFN)
                    t.wait_quad(dve, stored[s % 4], s // 4, 16, 0)
                    tt(y[:, s % 4], rec_b[:, DIM:2 * DIM], h2[:, s % 8], ALU.add).then_inc(y_ready, 1)
                if t.has(L_OUT):
                    s = t.slot(L_OUT)
                    t.wait(dve, h2_ready, L_OUT)
                    nc.vector.bn_stats(raw2[:, s % 2], h2[:, s % 8]).then_inc(raw2_ok, 1)
                if t.has(L_KEY):
                    s = t.slot(L_KEY)
                    q = s // QUAD
                    t.wait(dve, ksq_ready, L_KEY)
                    t.wait_quad(dve, newt, q - 2, NEWT, NEWT)
                    nc.vector.tensor_reduce(
                        sumsq[:, q % 2, (s % QUAD) * BLOCKS:(s % QUAD + 1) * BLOCKS],
                        key_sq[:, s % 2].rearrange("p (j n) -> p n j", n=BLOCKS), AX.X,
                        ALU.add).then_inc(sumsq_ok, 1)
                if t.has(L_OUT):
                    s = t.slot(L_OUT)
                    t.wait(dve, raw2_ok, L_OUT)
                    t.wait_quad(dve, ln2_step, s // QUAD - 2, 4, 4)
                    dve.sem_inc(dve_past, 1)
                    nc.vector.bn_aggr(stat2[:, s // QUAD % 2, s % QUAD], raw2[:, s % 2]).then_inc(stat2_ok, 1)
                q = t.quad(L_KEY - 4)
                if q is not None:
                    t.wait_quad(dve, newt, q, NEWT, NEWT)
                    t.wait(dve, nkey_ok, L_KEY - 4 - QUAD - 1)
                    nc.vector.reciprocal(nrecip[:, q % 2], nnorm[:]).then_inc(nrec_ok, 1)

            run(dve, turn)


def kernel(x, L0_tok_W1, L0_tok_b1, L0_tok_W2, L0_tok_b2, L0_attn_W_k, L0_attn_W_v, L0_attn_W_q,
           L0_ffn_W1, L0_ffn_b1, L0_ffn_W2, L0_ffn_b2):
    import numpy as np
    import concourse.bacc as bacc
    from concourse import mybir
    from concourse.bass_utils import run_bass_kernel_spmd

    rows = np.asarray(x).reshape(SLOTS, P, DIM)
    x_rows = rows.reshape(SLOTS // QUAD, QUAD, P, DIM).transpose(0, 2, 1, 3)
    x_cols = rows.reshape(SLOTS // QUAD, QUAD, P, KT, P).transpose(0, 4, 1, 3, 2)

    def jn(w):
        return np.asarray(w).reshape(BLOCKS, BLK, KT, P).transpose(3, 2, 1, 0).reshape(P, KT, DIM)

    arrays = {
        "x_rows": x_rows,
        "x_cols": x_cols,
        "tok_w1": np.asarray(L0_tok_W1).reshape(KT, P, HIDDEN).transpose(1, 0, 2),
        "tok_b1": np.asarray(L0_tok_b1).reshape(P, 1),
        "tok_w2": np.asarray(L0_tok_W2),
        "tok_b2": np.asarray(L0_tok_b2).reshape(1, 1),
        "w_k": jn(L0_attn_W_k),
        "w_q": jn(L0_attn_W_q),
        "w_v": np.asarray(L0_attn_W_v).reshape(DIM, KT, P).transpose(2, 1, 0),
        "ffn_w1": np.asarray(L0_ffn_W1).reshape(GROUPS, P, OT, DIM),
        "ffn_b1": np.asarray(L0_ffn_b1).reshape(GROUPS, P, OT),
        "ffn_w2": np.asarray(L0_ffn_W2).transpose(0, 2, 1).reshape(GROUPS, P, OT, DIM),
        "ffn_b2": np.asarray(L0_ffn_b2).reshape(GROUPS, KT, P).transpose(0, 2, 1),
    }
    arrays = {name: np.ascontiguousarray(a) for name, a in arrays.items()}
    nc = bacc.Bacc("TRN2", target_bir_lowering=False, num_devices=1)
    args = [nc.dram_tensor(name, a.shape, mybir.dt.float32, kind="ExternalInput").ap() for name, a in arrays.items()]
    out = nc.dram_tensor("out", (SLOTS, P, DIM), mybir.dt.float32, kind="ExternalOutput").ap()
    by_name = dict(zip(arrays, args))
    vit_tower_kernel(nc, out=out, **by_name)
    r = run_bass_kernel_spmd(nc, [arrays], core_ids=[0])
    return r.results[0]["out"].reshape(STEPS, BATCH, DIM)
```

```python
import concourse.bass as bass
from concourse import mybir
from contextlib import ExitStack

STEPS, BATCH, DIM = 16, 1024, 256
HIDDEN = 128
BLOCKS, BLK = 32, 8
GROUPS, INTER = 8, 1024
LN_EPS, NORM_EPS = 1e-5, 1e-6

P = 128
KT = DIM // P
SLOTS = STEPS * BATCH // P
LANES = BATCH // P
PER_GROUP = SLOTS // GROUPS
QUAD = 4
PLANE = BLOCKS * BLK
STATE = BLK * PLANE
HALF = STATE // 2
OT = INTER // P

L_XT = 25
L_TOK = 23
L_XW = 14
L_SOFT = 15
L_LN1 = 11
L_KEY = 9
L_SUM = 6
L_SEED = 5
L_NORM = 4
L_INV = 3
L_RET = 2
L_DEL = 1
L_UPD = 0
L_QRY = -1
L_OUT = -2
L_LN2 = -6
L_FFN = -8
L_WC = 6
WC_PLAN = {0: ("product", 0, 0), 1: ("product", 0, 1), 2: ("transpose", 0, None),
           4: ("product", 1, 0), 5: ("product", 1, 1), 6: ("transpose", 1, None)}
FIRST_TURN, LAST_TURN = -L_XT, SLOTS - 1 - L_FFN
LOOP_FROM = 11
LOOP_TURNS = 16
LOOP_COUNT = (SLOTS - L_XT - LOOP_FROM) // LOOP_TURNS
LOOP_TO = LOOP_FROM + LOOP_COUNT * LOOP_TURNS


def vit_tower_kernel(nc, x_rows, x_cols, tok_w1, tok_b1, tok_w2, tok_b2, w_k, w_q, w_v,
                     ffn_w1, ffn_w2, ffn_b2, out):
    f32 = mybir.dt.float32
    i32 = mybir.dt.int32
    ALU = mybir.AluOpType
    ACT = mybir.ActivationFunctionType
    AX = mybir.AxisListType

    ctx = ExitStack()
    with ctx:
        def sb(name, shape, dt=f32):
            return ctx.enter_context(nc.sbuf_tensor(name, shape, dt))

        def pb(name, shape):
            return ctx.enter_context(nc.psum_tensor(name, shape, f32))

        def sem(name):
            return ctx.enter_context(nc.semaphore(name))

        state = sb("state", [P, LANES, STATE])
        ret_prod = sb("ret_prod", [P, STATE])
        out_prod = sb("out_prod", [P, STATE])
        xt_in = sb("xt_in", [P, 2, QUAD, KT, P])
        x_in = sb("x_in", [P, 2, QUAD, DIM])
        xw = sb("xw", [P, 16, DIM])
        xn = sb("xn", [P, 2, DIM])
        xnT = sb("xnT", [P, 16, KT, P])
        key = sb("key", [P, 8, DIM])
        key_sq = sb("key_sq", [P, 8, DIM])
        nkey = sb("nkey", [P, 4, DIM])
        deltaT = sb("deltaT", [P, 2, KT, P])
        silu = sb("silu", [P, 2, DIM])
        outT = sb("outT", [P, 2, KT, P])
        h2 = sb("h2", [P, 8, DIM])
        xn2 = sb("xn2", [P, 2, DIM])
        xn2T = sb("xn2T", [P, 2, KT, P])
        th = sb("th", [P, QUAD, P])
        w1g = sb("w1g", [P, OT, DIM + 1])
        w2g = sb("w2g", [P, OT, DIM])
        b2g = sb("b2g", [P, KT])
        wcT_half = sb("wcT_half", [P, DIM])
        wc_next = sb("wc_next", [P, KT, DIM])
        bc_next = sb("bc_next", [P, KT])
        wc = sb("wc", [P, KT, DIM])
        bc = sb("bc", [P, KT, P])
        wk_s = sb("wk_s", [P, KT, DIM])
        wq_s = sb("wq_s", [P, KT, DIM])
        wv_s = sb("wv_s", [P, KT, DIM])
        tw1 = sb("tw1", [P, KT, HIDDEN])
        tb1 = sb("tb1", [P, 1])
        tw2 = sb("tw2", [P, 1])
        tb2 = sb("tb2", [P, 1])
        ident = sb("ident", [P, P])
        eul = sb("eul", [P, QUAD])
        mone = sb("mone", [P, QUAD])
        mhalf = sb("mhalf", [P, QUAD])
        energy = sb("energy", [P, 2, QUAD])
        sm = sb("sm", [P, 3, QUAD])
        weight = sb("weight", [P, 2, QUAD])
        sum1 = sb("sum1", [P, 2])
        dev1 = sb("dev1", [P, DIM])
        raw2 = sb("raw2", [P, 2, 6])
        nmean1 = sb("nmean1", [P, 2, QUAD])
        dev_sq1 = sb("dev_sq1", [P, 2, QUAD])
        stat2 = sb("stat2", [P, 2, QUAD, 2])
        ve1 = sb("ve1", [P, QUAD])
        ve2 = sb("ve2", [P, QUAD])
        mr2 = sb("mr2", [P, QUAD])
        rstd1 = sb("rstd1", [P, 2, QUAD])
        rstd2 = sb("rstd2", [P, 2, QUAD])
        shift1 = sb("shift1", [P, 2, QUAD])
        shift2 = sb("shift2", [P, 2, QUAD])
        QB = QUAD * BLOCKS
        sumsq = sb("sumsq", [P, 2, QB])
        root = sb("root", [P, 3, QB])
        nt = sb("nt", [P, 4, QB])
        nnorm = sb("nnorm", [P, QB])
        nrecip = sb("nrecip", [P, 2, QB])
        warm = sb("warm", [P, 1])

        upd = pb("upd", [P, STATE])
        del_b = pb("del_b", [P, 512])
        qry_b = pb("qry_b", [P, 512])
        rec_b = pb("rec_b", [P, 512])
        frt_b = pb("frt_b", [P, 512])

        setup_in = sem("setup_in")
        ident_ok = sem("ident_ok")
        warm_ok = sem("warm_ok")
        xt_loaded = [sem("xt_loaded0"), sem("xt_loaded1")]
        x_loaded = [sem("x_loaded0"), sem("x_loaded1")]
        group_in = sem("group_in")
        stored = [sem(f"stored{i}") for i in range(4)]
        tok_ready = sem("tok_ready")
        th_ready = sem("th_ready")
        en_ready = sem("en_ready")
        e_ready = sem("e_ready")
        sm_step = sem("sm_step")
        xw_ready = sem("xw_ready")
        nmean1_ok = sem("nmean1_ok")
        stat1_ok = sem("stat1_ok")
        ln1_step = sem("ln1_step")
        xn_ready = sem("xn_ready")
        tr_ready = sem("tr_ready")
        xnT_ready = sem("xnT_ready")
        xn2T_ready = sem("xn2T_ready")
        key_b_ready = sem("key_b_ready")
        key_ready = sem("key_ready")
        ksq_ready = sem("ksq_ready")
        sumsq_ok = sem("sumsq_ok")
        seed_sh = sem("seed_sh")
        seed_ok = sem("seed_ok")
        newt = sem("newt")
        NEWT = 12
        nrec_ok = sem("nrec_ok")
        nkey_ok = sem("nkey_ok")
        ret_done = sem("ret_done")
        dT_ready = sem("dT_ready")
        dT_out = sem("dT_out")
        del_ready = sem("del_ready")
        outer_done = sem("outer_done")
        sum_done = sem("sum_done")
        state_new = sem("state_new")
        qry_ready = sem("qry_ready")
        outp_done = sem("outp_done")
        sqT_ready = sem("sqT_ready")
        silu_ready = sem("silu_ready")
        outT_ready = sem("outT_ready")
        ik_ready = sem("ik_ready")
        h2_ready = sem("h2_ready")
        raw2_ok = sem("raw2_ok")
        stat2_ok = sem("stat2_ok")
        ln2_step = sem("ln2_step")
        xn2_ready = sem("xn2_ready")
        y_ready = sem("y_ready")
        part_b_ready = sem("part_b_ready")
        part_ready = sem("part_ready")
        PARTS, PARTS_OUT = len(WC_PLAN), len(WC_PLAN) + KT
        wc_ready = sem("wc_ready")

        gp_past = sem("gp_past")
        dve_past = sem("dve_past")

        block = ctx.enter_context(nc.Block())

        SETUP_DMAS = 8

        class Turn:

            def __init__(self, it, n):
                self.it, self.n, self.static = it, n, isinstance(it, int)

            def has(self, lead):
                return not self.static or 0 <= self.n + lead < SLOTS

            def slot(self, lead):
                return self.n + lead

            def wait(self, eng, s, lead, per=1, part=None, start=0):
                c = per * (self.n + lead - start) + (per if part is None else part)
                if self.static:
                    c = min(c, per * (SLOTS - start))
                self._wait(eng, s, per * 16, c)

            def quad(self, lead):
                n = self.n + lead
                return n // QUAD if n % QUAD == 0 and self.has(lead) else None

            def wait_quad(self, eng, s, q, per, part):
                c = per * q + part
                self._wait(eng, s, per * 4, c)

            def _wait(self, eng, s, per_turn, c):
                assert self.static or c > 0
                if c > 0 or not self.static:
                    eng.wait_ge(s, per_turn * self.it + c)

        def first_step(t, lead):
            return t.static and t.slot(lead) < LANES

        def early(t):
            return t.static and t.n < -L_UPD

        def scorer_bank(t):
            return upd[:, t.n % 2 * 512:(t.n % 2 + 1) * 512] if early(t) else frt_b[:]

        def key_bank(t):
            return qry_b if early(t) else frt_b

        def quads_over(n):
            return min(max((n + L_TOK) // QUAD, 0), SLOTS // QUAD)

        def parts_out(n):
            g, at = (n + L_WC) // PER_GROUP, (n + L_WC) % PER_GROUP
            done = sum(1 + (plan[2] == 1) for p, plan in WC_PLAN.items() if p <= at)
            return min(max(PARTS_OUT * g + done, 0), PARTS_OUT * GROUPS)

        def part_of(t):
            g, at = (t.n + L_WC) // PER_GROUP, (t.n + L_WC) % PER_GROUP
            if at not in WC_PLAN or (t.static and not 0 <= g < GROUPS):
                return g, 0, None
            return g, sum(p < at for p in WC_PLAN), WC_PLAN[at]

        def run(eng, turn):
            for n in range(FIRST_TURN, LOOP_FROM):
                turn(Turn(0, n))
            with eng.Fori(0, LOOP_COUNT) as it:
                for n in range(LOOP_FROM, LOOP_FROM + LOOP_TURNS):
                    turn(Turn(it, n))
            for n in range(LOOP_TO, LAST_TURN + 1):
                turn(Turn(0, n))

        def planes(ap):
            return ap.rearrange("p (j n i) -> p j n i", n=BLOCKS, i=BLK)

        @block.sync
        def _(sp):
            sp.dma_start(tw1[:], tok_w1).then_inc(setup_in, 16)
            sp.dma_start(tb1[:], tok_b1).then_inc(setup_in, 16)
            sp.dma_start(tw2[:], tok_w2).then_inc(setup_in, 16)
            sp.dma_start(tb2[:], tok_b2.broadcast_to([P, 1])).then_inc(setup_in, 16)

            def load_group(g):
                sp.dma_start(w1g[:], ffn_w1[g]).then_inc(group_in, 16)
                sp.dma_start(w2g[:], ffn_w2[g]).then_inc(group_in, 16)
                sp.dma_start(b2g[:], ffn_b2[g]).then_inc(group_in, 16)

            def turn(t):
                q = t.quad(L_XT)
                if q is not None:
                    t.wait(sp, tok_ready, L_XT - QUAD - 1)
                    sp.dma_start(xt_in[:, q % 2], x_cols[4 * t.it + q]).then_inc(xt_loaded[q % 2], 16)
                if t.n == FIRST_TURN:
                    sp.dma_start(wk_s[:], w_k).then_inc(setup_in, 16)
                    sp.dma_start(wq_s[:], w_q).then_inc(setup_in, 16)
                    sp.dma_start(wv_s[:], w_v).then_inc(setup_in, 16)
                    load_group(0)
                q = t.quad(L_XW + QUAD)
                if q is not None:
                    t.wait(sp, xw_ready, L_XW - 1)
                    sp.dma_start(x_in[:, q % 2], x_rows[4 * t.it + q]).then_inc(x_loaded[q % 2], 16)
                if t.n % PER_GROUP == 3 and 0 <= t.n // PER_GROUP < GROUPS - 1:
                    g = t.n // PER_GROUP + 1
                    sp.wait_ge(part_ready, PARTS_OUT * (t.it + g))
                    load_group(t.it + g)
                if t.has(L_FFN):
                    s = t.slot(L_FFN)
                    t.wait(sp, y_ready, L_FFN)
                    sp.dma_start(out[16 * t.it + s], h2[:, s % 8]).then_inc(stored[s % 4], 16)

            run(sp, turn)
            for i in range(4):
                sp.wait_ge(stored[i], 16 * SLOTS // 4)

        @block.gpsimd
        def _(gp):
            nc.gpsimd.memset(ident[:], 0.0).then_inc(ident_ok, 1)
            gp.wait_ge(ident_ok, 1)
            nc.gpsimd.affine_select(out=ident[:], in_=ident[:], compare_op=ALU.not_equal, fill=1.0, base=0,
                                    pattern=[[-1, P]], channel_multiplier=1).then_inc(ident_ok, 1)
            nc.gpsimd.memset(eul[:], 2.718281828459045).then_inc(ident_ok, 1)
            nc.gpsimd.memset(mone[:], -1.0).then_inc(ident_ok, 1)
            nc.gpsimd.memset(mhalf[:], -0.5).then_inc(ident_ok, 1)
            gp.wait_ge(ident_ok, 5)

            def layer_norm_1(t, q, lead):
                t.wait(gp, stat1_ok, lead + QUAD - 1)
                t.wait(gp, xn_ready, lead - QUAD - 1)
                gp.sem_inc(gp_past, 1)
                b = q % 2
                nc.gpsimd.tensor_scalar(ve1[:], dev_sq1[:, b], 1.0 / DIM, LN_EPS, ALU.mult,
                                        ALU.add).then_inc(ln1_step, 1)
                t.wait_quad(gp, ln1_step, q, 3, 1)
                nc.gpsimd.tensor_tensor(rstd1[:, b], ve1[:], mhalf[:], ALU.pow).then_inc(ln1_step, 1)
                t.wait_quad(gp, ln1_step, q, 3, 2)
                nc.gpsimd.tensor_tensor(shift1[:, b], nmean1[:, b], rstd1[:, b], ALU.mult).then_inc(ln1_step, 1)

            def layer_norm_2(t, q, lead):
                t.wait(gp, stat2_ok, lead + QUAD - 1)
                t.wait(gp, xn2_ready, lead - QUAD - 1)
                gp.sem_inc(gp_past, 1)
                b = q % 2
                nc.gpsimd.tensor_scalar(ve2[:], stat2[:, b, :, 1], 1.0, LN_EPS, ALU.mult,
                                        ALU.add).then_inc(ln2_step, 1)
                t.wait_quad(gp, ln2_step, q, 4, 1)
                nc.gpsimd.tensor_tensor(rstd2[:, b], ve2[:], mhalf[:], ALU.pow).then_inc(ln2_step, 1)
                t.wait_quad(gp, ln2_step, q, 4, 2)
                nc.gpsimd.tensor_tensor(mr2[:], stat2[:, b, :, 0], rstd2[:, b], ALU.mult).then_inc(ln2_step, 1)
                t.wait_quad(gp, ln2_step, q, 4, 3)
                gp.sem_inc(gp_past, 1)
                nc.gpsimd.tensor_scalar(shift2[:, b], mr2[:], -1.0, 0.0, ALU.mult, ALU.add).then_inc(ln2_step, 1)

            def square_sums(t, q):
                t.wait(gp, ksq_ready, L_SUM + QUAD - 1)
                sq = key_sq[:, (q % 2) * QUAD:(q % 2 + 1) * QUAD]
                for i, width in enumerate((DIM // 2, DIM // 4)):
                    nc.gpsimd.tensor_tensor(sq[:, :, 0:width], sq[:, :, 0:width], sq[:, :, width:2 * width],
                                            ALU.add).then_inc(sumsq_ok, 1)
                    t.wait_quad(gp, sumsq_ok, q, 3, i + 1)
                nc.gpsimd.tensor_tensor(sumsq[:, q % 2].rearrange("p (s n) -> p s n", n=BLOCKS), sq[:, :, 0:BLOCKS],
                                        sq[:, :, BLOCKS:2 * BLOCKS], ALU.add).then_inc(sumsq_ok, 1)

            def softmax(t, q):
                t.wait_quad(gp, e_ready, q, 1, 1)
                t.wait(gp, xw_ready, L_SOFT - QUAD - 1)
                b = q % 2
                nc.gpsimd.tensor_tensor(sm[:, 0], energy[:, b], energy[:, b], ALU.subtract).then_inc(sm_step, 1)
                t.wait_quad(gp, sm_step, q, 4, 1)
                nc.gpsimd.tensor_tensor(sm[:, 1], eul[:], sm[:, 0], ALU.pow).then_inc(sm_step, 1)
                t.wait_quad(gp, sm_step, q, 4, 2)
                nc.gpsimd.tensor_tensor(sm[:, 2], sm[:, 1], mone[:], ALU.pow).then_inc(sm_step, 1)
                t.wait_quad(gp, sm_step, q, 4, 3)
                nc.gpsimd.tensor_tensor(weight[:, b], sm[:, 1], sm[:, 2], ALU.mult).then_inc(sm_step, 1)

            def key_norm(t, q):
                b = q % 2
                s = sumsq[:, b]
                k = [0]

                tt, ts = nc.gpsimd.tensor_tensor, nc.gpsimd.tensor_scalar

                def step(op, dst, *args):
                    if op is ts:
                        gp.sem_inc(gp_past, 1)
                    op(dst, *args).then_inc(newt, 1)
                    k[0] += 1
                    if k[0] < NEWT:
                        t.wait_quad(gp, newt, q, NEWT, k[0])

                t.wait_quad(gp, seed_ok, q, 1, 1)
                step(tt, nt[:, 0], root[:, 0], root[:, 0], ALU.mult)
                step(tt, nt[:, 1], nt[:, 0], s, ALU.mult)
                step(ts, nt[:, 2], nt[:, 1], 0.375, -1.25, ALU.mult, ALU.add)
                step(tt, nt[:, 3], nt[:, 2], nt[:, 1], ALU.mult)
                step(ts, nt[:, 2], nt[:, 3], 1.0, 1.875, ALU.mult, ALU.add)
                step(tt, root[:, 1], root[:, 0], nt[:, 2], ALU.mult)
                step(tt, nt[:, 0], root[:, 1], root[:, 1], ALU.mult)
                step(tt, nt[:, 1], nt[:, 0], s, ALU.mult)
                step(ts, nt[:, 2], nt[:, 1], -0.5, 1.5, ALU.mult, ALU.add)
                step(tt, root[:, 2], root[:, 1], nt[:, 2], ALU.mult)
                step(tt, nt[:, 3], root[:, 2], s, ALU.mult)
                t.wait_quad(gp, nrec_ok, q - 1, 1, 1)
                step(ts, nnorm[:], nt[:, 3], -1.0, -NORM_EPS, ALU.mult, ALU.add)
                assert k[0] == NEWT

            def turn(t):
                if t.has(L_RET):
                    m = t.slot(L_RET)
                    q = m // QUAD
                    t.wait_quad(gp, nrec_ok, q, 1, 1)
                    t.wait(gp, key_ready, L_RET)
                    t.wait(gp, outer_done, L_RET - 4)
                    nc.gpsimd.tensor_tensor(
                        nkey[:, m % 4].rearrange("p (j n) -> p j n", n=BLOCKS),
                        key[:, m % 8].rearrange("p (j n) -> p j n", n=BLOCKS),
                        nrecip[:, q % 2, (m % QUAD) * BLOCKS:(m % QUAD + 1) * BLOCKS].unsqueeze(1)
                        .broadcast_to([P, BLK, BLOCKS]), ALU.mult).then_inc(nkey_ok, 1)
                if t.has(L_RET) and not first_step(t, L_RET):
                    t.wait(gp, nkey_ok, L_RET)
                    t.wait(gp, dT_ready, L_RET - 1)
                    for half in range(2):
                        t.wait(gp, state_new, L_RET - LANES, per=2, part=half + 1)
                        lo = half * HALF
                        nk = nkey[:, m % 4, half * P:(half + 1) * P]
                        nc.gpsimd.tensor_tensor(
                            ret_prod[:, lo:lo + HALF].rearrange("p (c i) -> p c i", i=BLK),
                            state[:, m % LANES, lo:lo + HALF].rearrange("p (c i) -> p c i", i=BLK),
                            nk.unsqueeze(2).broadcast_to([P, P, BLK]), ALU.mult).then_inc(ret_done, 1)
                q = t.quad(L_NORM)
                if q is not None:
                    key_norm(t, q)
                q = t.quad(L_SOFT)
                if q is not None:
                    softmax(t, q)
                q = t.quad(L_LN1)
                if q is not None:
                    layer_norm_1(t, q, L_LN1)
                q = t.quad(L_LN2)
                if q is not None:
                    layer_norm_2(t, q, L_LN2)
                q = t.quad(L_SUM)
                if q is not None:
                    square_sums(t, q)

            run(gp, turn)

        @block.tensor
        def _(pe):
            mm = nc.tensor.matmul

            def tr(dst, src, start=False, stop=False):
                return mm(dst, src, ident[:], start=start, stop=stop, is_transpose=True, skip_group_check=True)

            def plane_sums(prod, dst, done, t, lead, start, from_slot=0):
                for j in range(BLK):
                    if j % (BLK // 2) == 0:
                        t.wait(pe, done, lead, per=2, part=j // (BLK // 2) + 1, start=from_slot)
                    for h in range(KT):
                        col = j * PLANE + h * P
                        last = tr(dst[:, h * P:(h + 1) * P], prod[:, col:col + P],
                                  start=start and j == 0 and h == 0, stop=(j == BLK - 1))
                return last

            def scorer_read(t, back):
                t.wait(pe, th_ready, L_TOK - back)
                if not t.has(L_TOK - back):
                    pe.wait_ge(e_ready, quads_over(t.n - back))
                    pe.wait_ge(part_ready, parts_out(t.n - back))

            def turn(t):
                if t.has(L_OUT):
                    t.wait(pe, dT_out, L_DEL - 1)
                    plane_sums(out_prod, rec_b, outp_done, t, L_OUT, start=True).then_inc(sqT_ready, 1)
                if t.has(L_KEY) or t.has(L_FFN):
                    if early(t):
                        t.wait(pe, xnT_ready, L_KEY - 1)
                    else:
                        t.wait(pe, ksq_ready, L_KEY - 1)
                    if not t.has(L_KEY - 1):
                        t.wait(pe, xn2T_ready, L_FFN - 1)
                        scorer_read(t, 1)
                    if t.has(L_KEY):
                        s = t.slot(L_KEY)
                        t.wait(pe, xn_ready, L_KEY)
                        for k in range(KT):
                            last = tr(frt_b[:, k * P:(k + 1) * P], xn[:, s % 2, k * P:(k + 1) * P],
                                      start=(k == 0), stop=True)
                    if t.has(L_FFN):
                        s = t.slot(L_FFN)
                        t.wait(pe, xn2_ready, L_FFN)
                        for k in range(KT):
                            last = tr(frt_b[:, DIM + k * P:DIM + (k + 1) * P], xn2[:, s % 2, k * P:(k + 1) * P],
                                      start=(k == 0 and not t.has(L_KEY)), stop=True)
                    last.then_inc(tr_ready, 1)
                if t.has(L_QRY):
                    s = t.slot(L_QRY)
                    t.wait(pe, outp_done, L_QRY - 1, per=2)
                    for k in range(KT):
                        last = mm(qry_b[:, 0:DIM], xnT[:, s % 16, k, :], wq_s[:, k, :], start=(k == 0),
                                  stop=(k == KT - 1))
                    last.then_inc(qry_ready, 1)
                if t.has(L_OUT) or t.has(L_FFN):
                    t.wait(pe, outer_done, L_UPD)
                    if t.has(L_OUT):
                        s = t.slot(L_OUT)
                        t.wait(pe, outT_ready, L_OUT)
                        for h in range(KT):
                            last = tr(del_b[:, h * P:(h + 1) * P], outT[:, s % 2, h, :], start=(h == 0), stop=True)
                    if t.has(L_FFN):
                        s = t.slot(L_FFN)
                        if not t.has(L_DEL - 1):
                            t.wait(pe, h2_ready, L_OUT - 1)
                            t.wait(pe, y_ready, L_FFN - 1)
                        t.wait(pe, xn2T_ready, L_FFN)
                        if s % PER_GROUP == 0:
                            pe.wait_ge(wc_ready, 2 * (t.it + s // PER_GROUP + 1))
                        for k in range(KT):
                            mm(del_b[:, DIM:2 * DIM], xn2T[:, s % 2, k, :], wc[:, k, :],
                               start=(k == 0 and not t.has(L_OUT)), stop=False, skip_group_check=True)
                        for h in range(KT):
                            last = tr(del_b[:, DIM + h * P:DIM + (h + 1) * P], bc[:, h, :], stop=True)
                    last.then_inc(ik_ready, 1)
                g, part, plan = part_of(t)
                q = t.n + L_TOK - QUAD
                quad_over = q % QUAD == 0 and t.has(L_TOK - QUAD)
                opened = False
                if quad_over or t.has(L_TOK) or plan:
                    if t.n == -L_TOK:
                        pe.wait_ge(setup_in, 16 * 7)
                        pe.wait_ge(ident_ok, 2)
                    if early(t):
                        scorer_read(t, 2)
                    else:
                        t.wait(pe, xnT_ready, L_KEY)
                        t.wait(pe, xn2T_ready, L_FFN)
                bank = scorer_bank(t)
                if plan:
                    kind, h, c = plan
                    if part == 0:
                        pe.wait_ge(group_in, 48 * (t.it + g + 1))
                    if kind == "product":
                        for o in range(OT):
                            last = mm(bank[:, DIM:DIM + P + c], w2g[:, o, h * P:(h + 1) * P],
                                      w1g[:, o, c * P:(c + 1) * P + c], start=(o == 0), stop=(o == OT - 1),
                                      skip_group_check=True)
                    else:
                        pe.wait_ge(part_ready, PARTS_OUT * (t.it + g) + (h + 1) * PARTS_OUT // KT - 1)
                        for k in range(KT):
                            last = tr(bank[:, DIM + k * P:DIM + (k + 1) * P], wcT_half[:, k * P:(k + 1) * P],
                                      start=(k == 0), stop=True)
                    opened = True
                    last.then_inc(part_b_ready, 1)
                if quad_over:
                    pe.wait_ge(th_ready, 16 * t.it + q + QUAD)
                    for i in range(QUAD):
                        last = mm(bank[:, P + i:P + i + 1], th[:, i, :], tw2[:],
                                  start=(i == 0 and not opened), stop=True, skip_group_check=True)
                    opened = True
                    last.then_inc(en_ready, 1)
                if t.has(L_TOK):
                    s = t.slot(L_TOK)
                    if s % QUAD == 0:
                        pe.wait_ge(xt_loaded[s // QUAD % 2], 32 * t.it + 16 * (s // QUAD // 2 + 1))
                    for k in range(KT):
                        last = mm(bank[:, 0:P], tw1[:, k, :], xt_in[:, s // QUAD % 2, s % QUAD, k, :],
                                  start=(k == 0 and not opened), stop=(k == KT - 1), skip_group_check=True)
                    last.then_inc(tok_ready, 1)
                if t.has(L_DEL):
                    s = t.slot(L_DEL)
                    t.wait(pe, outT_ready, L_OUT)
                    for h in range(KT):
                        for k in range(KT):
                            last = mm(rec_b[:, h * P:(h + 1) * P], wv_s[:, k, h * P:(h + 1) * P], xnT[:, s % 16, k, :],
                               start=(h == 0 and k == 0), stop=(first_step(t, L_DEL) and k == KT - 1),
                               skip_group_check=True)
                    if not first_step(t, L_DEL):
                        last = plane_sums(ret_prod, rec_b, ret_done, t, L_DEL, start=False, from_slot=LANES)
                    last.then_inc(dT_ready, 1)
                if t.has(L_KEY):
                    s = t.slot(L_KEY)
                    t.wait(pe, xnT_ready, L_KEY)
                    t.wait(pe, xn2T_ready, L_FFN)
                    if early(t):
                        t.wait(pe, ksq_ready, L_KEY - 1)
                    else:
                        scorer_read(t, 0)
                    for k in range(KT):
                        last = mm(key_bank(t)[:, 0:DIM], xnT[:, s % 16, k, :], wk_s[:, k, :], start=(k == 0),
                                  stop=(k == KT - 1))
                    last.then_inc(key_b_ready, 1)
                if t.has(L_DEL):
                    s = t.slot(L_DEL)
                    t.wait(pe, dT_out, L_DEL)
                    t.wait(pe, outer_done, L_DEL - 1)
                    t.wait(pe, h2_ready, L_OUT)
                    t.wait(pe, y_ready, L_FFN)
                    for h in range(KT):
                        last = tr(del_b[:, h * P:(h + 1) * P], deltaT[:, s % 2, h, :], start=(h == 0), stop=True)
                    last.then_inc(del_ready, 1)

            run(pe, turn)

        @block.scalar
        def _(act):
            fn = nc.scalar.activation
            act.wait_ge(ident_ok, 2)
            fn(warm[:], ident[:, 0:1], ACT.Silu).then_inc(warm_ok, 1)

            def normalise(t):
                if t.has(L_KEY):
                    s = t.slot(L_KEY)
                    qp = s // QUAD % 2
                    t.wait_quad(act, ln1_step, s // QUAD, 3, 3)
                    fn(xn[:, s % 2], xw[:, s % 16], ACT.Identity, scale=rstd1[:, qp, s % QUAD:s % QUAD + 1],
                       bias=shift1[:, qp, s % QUAD:s % QUAD + 1]).then_inc(xn_ready, 1)
                if t.has(L_FFN):
                    s = t.slot(L_FFN)
                    qp = s // QUAD % 2
                    t.wait_quad(act, ln2_step, s // QUAD, 4, 4)
                    fn(xn2[:, s % 2], h2[:, s % 8], ACT.Identity, scale=rstd2[:, qp, s % QUAD:s % QUAD + 1],
                       bias=shift2[:, qp, s % QUAD:s % QUAD + 1]).then_inc(xn2_ready, 1)

            def scorer(t):
                g, part, plan = part_of(t)
                q = t.n + L_TOK - QUAD
                quad_over = q % QUAD == 0 and t.has(L_TOK - QUAD)
                if plan or quad_over or t.has(L_TOK):
                    if t.n == -L_TOK:
                        act.wait_ge(setup_in, 16 * 7)
                    if plan:
                        act.wait_ge(part_b_ready, PARTS * (t.it + g) + part + 1)
                    if quad_over:
                        act.wait_ge(en_ready, 4 * t.it + q // QUAD + 1)
                    t.wait(act, tok_ready, L_TOK)
                bank = scorer_bank(t)
                if plan:
                    kind, h, c = plan
                    if part == 0 and (not t.static or g > 0):
                        act.wait_ge(wc_ready, 2 * (t.it + g))
                    if kind == "product":
                        fn(wcT_half[:, c * P:(c + 1) * P], bank[:, DIM:DIM + P], ACT.Copy).then_inc(part_ready, 1)
                        if c == 1:
                            fn(bc_next[:, h:h + 1], bank[:, DIM + P:DIM + P + 1], ACT.Identity,
                               bias=b2g[:, h:h + 1]).then_inc(part_ready, 1)
                    else:
                        fn(wc_next[:, :, h * P:(h + 1) * P],
                           bank[:, DIM:2 * DIM].rearrange("p (k c) -> p k c", k=KT), ACT.Copy).then_inc(part_ready, 1)
                if quad_over:
                    t.wait_quad(act, sm_step, q // QUAD - 2, 4, 4)
                    fn(energy[:, q // QUAD % 2], bank[:, P:P + QUAD], ACT.Identity, bias=tb2[:]).then_inc(e_ready, 1)
                if t.has(L_TOK):
                    s = t.slot(L_TOK)
                    fn(th[:, s % QUAD], bank[:, 0:P], ACT.Tanh, bias=tb1[:]).then_inc(th_ready, 1)

            def turn(t):
                if not early(t):
                    normalise(t)
                if t.has(L_FFN) and t.slot(L_FFN) % PER_GROUP == 0:
                    g = t.slot(L_FFN) // PER_GROUP
                    act.wait_ge(part_ready, PARTS_OUT * (t.it + g + 1))
                    t.wait(act, y_ready, L_FFN - 1)
                    fn(wc[:], wc_next[:], ACT.Copy).then_inc(wc_ready, 1)
                    fn(bc[:], bc_next[:].unsqueeze(2).broadcast_to([P, KT, P]), ACT.Copy).then_inc(wc_ready, 1)
                if t.has(L_OUT):
                    s = t.slot(L_OUT)
                    t.wait(act, sqT_ready, L_OUT)
                    fn(silu[:, s % 2], rec_b[:, 0:DIM], ACT.Silu).then_inc(silu_ready, 1)
                if t.has(L_KEY) or t.has(L_FFN):
                    act.wait_ge(tr_ready, 16 * t.it + t.n + L_KEY + 1)
                    if t.has(L_FFN):
                        s = t.slot(L_FFN)
                        fn(xn2T[:, s % 2].rearrange("p k b -> p (k b)"), frt_b[:, DIM:2 * DIM],
                           ACT.Copy).then_inc(xn2T_ready, 1)
                    if t.has(L_KEY):
                        s = t.slot(L_KEY)
                        t.wait(act, qry_ready, L_KEY - 16)
                        fn(xnT[:, s % 16].rearrange("p k b -> p (k b)"), frt_b[:, 0:DIM],
                           ACT.Copy).then_inc(xnT_ready, 1)
                for half in range(2):
                    if half == 1:
                        scorer(t)
                    if t.has(L_UPD):
                        s = t.slot(L_UPD)
                        lo = half * HALF
                        if first_step(t, L_UPD):
                            t.wait(act, outer_done, L_UPD)
                            fn(state[:, s % LANES, lo:lo + HALF], upd[:, lo:lo + HALF], ACT.Tanh,
                               scale=-1.0).then_inc(state_new, 1)
                        else:
                            t.wait(act, sum_done, L_UPD, per=2, part=half + 1, start=LANES)
                            fn(state[:, s % LANES, lo:lo + HALF], upd[:, lo:lo + HALF],
                               ACT.Tanh).then_inc(state_new, 1)
                if t.has(L_XW):
                    s = t.slot(L_XW)
                    qp, i = s // QUAD % 2, s % QUAD
                    if i == 0:
                        act.wait_ge(x_loaded[qp], 32 * t.it + 16 * (s // QUAD // 2 + 1))
                        t.wait_quad(act, sm_step, s // QUAD, 4, 4)
                        t.wait_quad(act, ln1_step, s // QUAD - 2, 3, 3)
                    t.wait(act, h2_ready, L_XW - 16)
                    fn(xw[:, s % 16], x_in[:, qp, i], ACT.Copy, scale=weight[:, qp, i:i + 1],
                       accum_out=sum1[:, s % 2:s % 2 + 1]).then_inc(xw_ready, 1)
                    t.wait(act, xw_ready, L_XW)
                    fn(nmean1[:, qp, i:i + 1], sum1[:, s % 2:s % 2 + 1], ACT.Copy,
                       scale=-1.0 / DIM).then_inc(nmean1_ok, 1)
                if t.has(L_DEL):
                    s = t.slot(L_DEL)
                    t.wait(act, dT_ready, L_DEL)
                    fn(deltaT[:, s % 2].rearrange("p h b -> p (h b)"), rec_b[:, 0:DIM], ACT.Copy).then_inc(dT_out, 1)
                if t.has(L_XW):
                    s = t.slot(L_XW)
                    qp, i = s // QUAD % 2, s % QUAD
                    t.wait(act, nmean1_ok, L_XW)
                    t.wait(act, stat1_ok, L_XW - 1)
                    fn(dev1[:], xw[:, s % 16], ACT.Square, bias=nmean1[:, qp, i:i + 1],
                       accum_out=dev_sq1[:, qp, i:i + 1]).then_inc(stat1_ok, 1)
                if t.static and early(Turn(0, t.n + 1)):
                    normalise(Turn(0, t.n + 1))
                if t.has(L_KEY):
                    s = t.slot(L_KEY)
                    t.wait(act, key_b_ready, L_KEY)
                    t.wait(act, nkey_ok, L_KEY - 8)
                    bank = key_bank(t)
                    fn(key[:, s % 8], bank[:, 0:DIM], ACT.Copy).then_inc(key_ready, 1)
                    if s % QUAD == 0:
                        t.wait_quad(act, sumsq_ok, s // QUAD - 2, 3, 3)
                    fn(key_sq[:, s % 8], bank[:, 0:DIM], ACT.Square).then_inc(ksq_ready, 1)

            run(act, turn)

        @block.vector
        def _(dve):
            tt = nc.vector.tensor_tensor

            def turn(t):
                if t.has(L_UPD):
                    s = t.slot(L_UPD)
                    t.wait(dve, nkey_ok, L_UPD)
                    t.wait(dve, del_ready, L_UPD)
                    nk = nkey[:, s % 4].rearrange("p (j n) -> p j n", n=BLOCKS)
                    delta = del_b[:, 0:DIM].rearrange("p (n i) -> p n i", i=BLK)
                    t.wait(dve, state_new, L_UPD - 1, per=2)
                    tt(planes(upd[:]), delta.unsqueeze(1).broadcast_to([P, BLK, BLOCKS, BLK]),
                       nk.unsqueeze(3).broadcast_to([P, BLK, BLOCKS, BLK]), ALU.mult).then_inc(outer_done, 1)
                if t.has(L_OUT):
                    s = t.slot(L_OUT)
                    t.wait(dve, silu_ready, L_OUT)
                    tt(outT[:, s % 2].rearrange("p h b -> p (h b)"), rec_b[:, 0:DIM], silu[:, s % 2],
                       ALU.mult).then_inc(outT_ready, 1)
                if t.has(L_UPD):
                    s = t.slot(L_UPD)
                    for half in range(0 if first_step(t, L_UPD) else 2):
                        lo = half * HALF
                        t.wait(dve, outer_done, L_UPD)
                        tt(upd[:, lo:lo + HALF], state[:, s % LANES, lo:lo + HALF], upd[:, lo:lo + HALF],
                           ALU.subtract).then_inc(sum_done, 1)
                if t.has(L_OUT) or t.has(L_FFN):
                    dve.wait_ge(ik_ready, 16 * t.it + t.n + L_OUT + 1)
                if t.has(L_OUT):
                    s = t.slot(L_OUT)
                    t.wait_quad(dve, stored[s % 4], (s - 8) // 4, 16, 16)
                    tt(h2[:, s % 8], del_b[:, 0:DIM], xw[:, s % 16], ALU.add).then_inc(h2_ready, 1)
                if t.has(L_FFN):
                    s = t.slot(L_FFN)
                    tt(h2[:, s % 8], del_b[:, DIM:2 * DIM], h2[:, s % 8], ALU.add).then_inc(y_ready, 1)
                if t.has(L_OUT):
                    s = t.slot(L_OUT)
                    t.wait(dve, h2_ready, L_OUT)
                    nc.vector.bn_stats(raw2[:, s % 2], h2[:, s % 8]).then_inc(raw2_ok, 1)
                if t.has(L_QRY):
                    s = t.slot(L_QRY)
                    t.wait(dve, qry_ready, L_QRY)
                    t.wait(dve, sqT_ready, L_QRY - 1)
                    for half in range(2):
                        lo = half * HALF
                        t.wait(dve, state_new, L_QRY, per=2, part=half + 1)
                        tt(out_prod[:, lo:lo + HALF].rearrange("p (c i) -> p c i", i=BLK),
                           state[:, s % LANES, lo:lo + HALF].rearrange("p (c i) -> p c i", i=BLK),
                           qry_b[:, half * P:(half + 1) * P].unsqueeze(2).broadcast_to([P, P, BLK]),
                           ALU.mult).then_inc(outp_done, 1)
                if t.has(L_OUT):
                    s = t.slot(L_OUT)
                    t.wait(dve, raw2_ok, L_OUT)
                    if s % QUAD == 0:
                        t.wait_quad(dve, ln2_step, s // QUAD - 2, 4, 4)
                    dve.sem_inc(dve_past, 1)
                    nc.vector.bn_aggr(stat2[:, s // QUAD % 2, s % QUAD], raw2[:, s % 2]).then_inc(stat2_ok, 1)
                q = t.quad(L_INV)
                if q is not None:
                    t.wait_quad(dve, newt, q, NEWT, NEWT)
                    t.wait(dve, nkey_ok, L_INV - QUAD - 1)
                    nc.vector.reciprocal(nrecip[:, q % 2], nnorm[:]).then_inc(nrec_ok, 1)
                q = t.quad(L_SEED)
                if q is not None:
                    t.wait_quad(dve, sumsq_ok, q, 3, 3)
                    t.wait_quad(dve, newt, q - 1, NEWT, NEWT)
                    nc.vector.tensor_scalar(nt[:, 3].bitcast(i32), sumsq[:, q % 2].bitcast(i32), 1, None,
                                            ALU.logical_shift_right).then_inc(seed_sh, 1)
                    t.wait_quad(dve, seed_sh, q, 1, 1)
                    nc.vector.tensor_scalar(root[:, 0].bitcast(i32), nt[:, 3].bitcast(i32), -1.0, float(0x5f3759df),
                                            ALU.mult, ALU.add).then_inc(seed_ok, 1)

            run(dve, turn)


def kernel(x, L0_tok_W1, L0_tok_b1, L0_tok_W2, L0_tok_b2, L0_attn_W_k, L0_attn_W_v, L0_attn_W_q,
           L0_ffn_W1, L0_ffn_b1, L0_ffn_W2, L0_ffn_b2):
    import numpy as np
    import concourse.bacc as bacc
    from concourse import mybir
    from concourse.bass_utils import run_bass_kernel_spmd

    rows = np.asarray(x).reshape(SLOTS, P, DIM)
    x_rows = rows.reshape(SLOTS // QUAD, QUAD, P, DIM).transpose(0, 2, 1, 3)
    x_cols = rows.reshape(SLOTS // QUAD, QUAD, P, KT, P).transpose(0, 4, 1, 3, 2)

    def jn(w):
        return np.asarray(w).reshape(BLOCKS, BLK, KT, P).transpose(3, 2, 1, 0).reshape(P, KT, DIM)

    arrays = {
        "x_rows": x_rows,
        "x_cols": x_cols,
        "tok_w1": np.asarray(L0_tok_W1).reshape(KT, P, HIDDEN).transpose(1, 0, 2),
        "tok_b1": np.asarray(L0_tok_b1).reshape(P, 1),
        "tok_w2": np.asarray(L0_tok_W2),
        "tok_b2": np.asarray(L0_tok_b2).reshape(1, 1),
        "w_k": jn(L0_attn_W_k),
        "w_q": jn(L0_attn_W_q),
        "w_v": np.asarray(L0_attn_W_v).reshape(DIM, KT, P).transpose(2, 1, 0),
        "ffn_w1": np.concatenate([np.asarray(L0_ffn_W1).reshape(GROUPS, P, OT, DIM),
                                  np.asarray(L0_ffn_b1).reshape(GROUPS, P, OT, 1)], axis=3),
        "ffn_w2": np.asarray(L0_ffn_W2).transpose(0, 2, 1).reshape(GROUPS, P, OT, DIM),
        "ffn_b2": np.asarray(L0_ffn_b2).reshape(GROUPS, KT, P).transpose(0, 2, 1),
    }
    arrays = {name: np.ascontiguousarray(a) for name, a in arrays.items()}
    nc = bacc.Bacc("TRN2", target_bir_lowering=False, num_devices=1)
    args = [nc.dram_tensor(name, a.shape, mybir.dt.float32, kind="ExternalInput").ap() for name, a in arrays.items()]
    out = nc.dram_tensor("out", (SLOTS, P, DIM), mybir.dt.float32, kind="ExternalOutput").ap()
    by_name = dict(zip(arrays, args))
    vit_tower_kernel(nc, out=out, **by_name)
    r = run_bass_kernel_spmd(nc, [arrays], core_ids=[0])
    return r.results[0]["out"].reshape(STEPS, BATCH, DIM)
```

```python
import concourse.bass as bass
from concourse import mybir
from contextlib import ExitStack

STEPS, BATCH, DIM = 16, 1024, 256
HIDDEN = 128
BLOCKS, BLK = 32, 8
GROUPS, INTER = 8, 1024
LN_EPS, NORM_EPS = 1e-5, 1e-6

P = 128
KT = DIM // P
SLOTS = STEPS * BATCH // P
LANES = BATCH // P
PER_GROUP = SLOTS // GROUPS
QUAD = 4
PLANE = BLOCKS * BLK
STATE = BLK * PLANE
HALF = STATE // 2
OT = INTER // P

L_XT = 25
L_TOK = 23
L_SOFT = 17
L_XW = 14
L_LN1 = 11
L_KEY = 9
L_SUM = 6
L_SEED = 5
L_NORM = 4
L_INV = 3
L_RET = 2
L_DEL = 1
L_UPD = 0
L_QRY = -1
L_OUT = -2
L_STAT2 = -3
L_LN2 = -6
L_FFN = -8
L_WC = 6
WC_PLAN = {0: ("product", 0, 0), 1: ("product", 0, 1), 2: ("transpose", 0, None),
           4: ("product", 1, 0), 5: ("product", 1, 1), 6: ("transpose", 1, None)}
FIRST_TURN, LAST_TURN = -L_XT, SLOTS - 1 - L_FFN
LOOP_FROM = 11
LOOP_TURNS = 16
LOOP_COUNT = (SLOTS - L_XT - LOOP_FROM) // LOOP_TURNS
LOOP_TO = LOOP_FROM + LOOP_COUNT * LOOP_TURNS


def vit_tower_kernel(nc, x_rows, x_cols, tok_w1, tok_b1, tok_w2, tok_b2, w_k, w_q, w_v,
                     ffn_w1, ffn_w2, ffn_b2, out):
    f32 = mybir.dt.float32
    i32 = mybir.dt.int32
    ALU = mybir.AluOpType
    ACT = mybir.ActivationFunctionType

    ctx = ExitStack()
    with ctx:
        def sb(name, shape, dt=f32):
            return ctx.enter_context(nc.sbuf_tensor(name, shape, dt))

        def pb(name, shape):
            return ctx.enter_context(nc.psum_tensor(name, shape, f32))

        def sem(name):
            return ctx.enter_context(nc.semaphore(name))

        state = sb("state", [P, LANES, STATE])
        ret_prod = sb("ret_prod", [P, STATE])
        out_prod = sb("out_prod", [P, STATE])
        xt_in = sb("xt_in", [P, 2, QUAD, KT, P])
        x_in = sb("x_in", [P, 2, QUAD, DIM])
        xw = sb("xw", [P, 16, DIM])
        xn = sb("xn", [P, 2, DIM])
        xnT = sb("xnT", [P, 16, KT, P])
        key = sb("key", [P, 8, DIM])
        key_sq = sb("key_sq", [P, 8, DIM])
        nkey = sb("nkey", [P, 4, DIM])
        deltaT = sb("deltaT", [P, 2, KT, P])
        silu = sb("silu", [P, 2, DIM])
        outT = sb("outT", [P, 2, KT, P])
        h2 = sb("h2", [P, 8, DIM])
        xn2 = sb("xn2", [P, 2, DIM])
        xn2T = sb("xn2T", [P, 2, KT, P])
        th = sb("th", [P, QUAD, P])
        w1g = sb("w1g", [P, OT, DIM + 1])
        w2g = sb("w2g", [P, OT, DIM])
        b2g = sb("b2g", [P, KT])
        wcT_half = sb("wcT_half", [P, DIM])
        wc_next = sb("wc_next", [P, KT, DIM])
        bc_next = sb("bc_next", [P, DIM])
        bc_col = sb("bc_col", [P, KT])
        wc = sb("wc", [P, KT, DIM])
        bc = sb("bc", [P, DIM])
        wk_s = sb("wk_s", [P, KT, DIM])
        wq_s = sb("wq_s", [P, KT, DIM])
        wv_s = sb("wv_s", [P, KT, DIM])
        tw1 = sb("tw1", [P, KT, HIDDEN])
        tb1 = sb("tb1", [P, 1])
        tw2 = sb("tw2", [P, 1])
        tb2 = sb("tb2", [P, 1])
        ident = sb("ident", [P, P])
        eul = sb("eul", [P, QUAD])
        mone = sb("mone", [P, QUAD])
        mhalf = sb("mhalf", [P, QUAD])
        energy = sb("energy", [P, 2, QUAD])
        sm = sb("sm", [P, 3, QUAD])
        weight = sb("weight", [P, 2, QUAD])
        sum1 = sb("sum1", [P, 2])
        dev = sb("dev", [P, DIM])
        nmean1 = sb("nmean1", [P, 2, QUAD])
        dev_sq1 = sb("dev_sq1", [P, 2, QUAD])
        sum2 = sb("sum2", [P, 2])
        nmean2 = sb("nmean2", [P, 2, QUAD])
        dev_sq2 = sb("dev_sq2", [P, 2, QUAD])
        ve1 = sb("ve1", [P, QUAD])
        ve2 = sb("ve2", [P, QUAD])
        rstd1 = sb("rstd1", [P, 2, QUAD])
        rstd2 = sb("rstd2", [P, 2, QUAD])
        shift1 = sb("shift1", [P, 2, QUAD])
        shift2 = sb("shift2", [P, 2, QUAD])
        QB = QUAD * BLOCKS
        sumsq = sb("sumsq", [P, 2, QB])
        root = sb("root", [P, 2, QB])
        nt = sb("nt", [P, 4, QB])
        nnorm = sb("nnorm", [P, QB])
        nrecip = sb("nrecip", [P, 2, QB])
        warm = sb("warm", [P, 1])

        upd = pb("upd", [P, STATE])
        del_b = pb("del_b", [P, 512])
        qry_b = pb("qry_b", [P, 512])
        rec_b = pb("rec_b", [P, 512])
        frt_b = pb("frt_b", [P, 512])

        scorer_in = sem("scorer_in")
        attn_in = sem("attn_in")
        ident_ok = sem("ident_ok")
        warm_ok = sem("warm_ok")
        xt_loaded = [sem("xt_loaded0"), sem("xt_loaded1")]
        x_loaded = [sem("x_loaded0"), sem("x_loaded1")]
        group_in = sem("group_in")
        stored = [sem(f"stored{i}") for i in range(4)]
        tok_ready = sem("tok_ready")
        th_ready = sem("th_ready")
        en_ready = sem("en_ready")
        e_ready = sem("e_ready")
        sm_step = sem("sm_step")
        xw_ready = sem("xw_ready")
        nmean1_ok = sem("nmean1_ok")
        stat1_ok = sem("stat1_ok")
        ln1_step = sem("ln1_step")
        xn_ready = sem("xn_ready")
        tr_ready = sem("tr_ready")
        xnT_ready = sem("xnT_ready")
        xn2T_ready = sem("xn2T_ready")
        key_b_ready = sem("key_b_ready")
        key_ready = sem("key_ready")
        ksq_ready = sem("ksq_ready")
        sumsq_ok = sem("sumsq_ok")
        seed_sh = sem("seed_sh")
        seed_ok = sem("seed_ok")
        newt = sem("newt")
        NEWT = 9
        nnorm_ok = sem("nnorm_ok")
        nrec_ok = sem("nrec_ok")
        nkey_ok = sem("nkey_ok")
        ret_done = sem("ret_done")
        dT_ready = sem("dT_ready")
        dT_out = sem("dT_out")
        del_ready = sem("del_ready")
        outer_done = sem("outer_done")
        sum_done = sem("sum_done")
        state_new = sem("state_new")
        qry_ready = sem("qry_ready")
        outp_done = sem("outp_done")
        folded = sem("folded")
        sqT_ready = sem("sqT_ready")
        silu_ready = sem("silu_ready")
        outT_ready = sem("outT_ready")
        ik_ready = sem("ik_ready")
        h2_ready = sem("h2_ready")
        sum2_ok = sem("sum2_ok")
        nmean2_ok = sem("nmean2_ok")
        stat2_ok = sem("stat2_ok")
        ln2_step = sem("ln2_step")
        xn2_ready = sem("xn2_ready")
        y_ready = sem("y_ready")
        biased = sem("biased")
        part_b_ready = sem("part_b_ready")
        part_ready = sem("part_ready")
        PARTS, PARTS_OUT = len(WC_PLAN), len(WC_PLAN) + 2 * KT
        wc_ready = sem("wc_ready")
        bc_ready = sem("bc_ready")

        gp_past = sem("gp_past")

        block = ctx.enter_context(nc.Block())

        SCORER_DMAS, ATTN_DMAS, GROUP_DMAS = 4, 3, 3

        class Turn:

            def __init__(self, it, n):
                self.it, self.n, self.static = it, n, isinstance(it, int)

            def has(self, lead):
                return not self.static or 0 <= self.n + lead < SLOTS

            def slot(self, lead):
                return self.n + lead

            def wait(self, eng, s, lead, per=1, part=None, start=0):
                c = per * (self.n + lead - start) + (per if part is None else part)
                if self.static:
                    c = min(c, per * (SLOTS - start))
                self._wait(eng, s, per * 16, c)

            def quad(self, lead):
                n = self.n + lead
                return n // QUAD if n % QUAD == 0 and self.has(lead) else None

            def wait_quad(self, eng, s, q, per, part):
                c = per * q + part
                self._wait(eng, s, per * 4, c)

            def _wait(self, eng, s, per_turn, c):
                assert self.static or c > 0
                if c > 0 or not self.static:
                    eng.wait_ge(s, per_turn * self.it + c)

        def first_step(t, lead):
            return t.static and t.slot(lead) < LANES

        def early(t):
            return t.static and t.n < -L_UPD

        def scorer_bank(t):
            return upd[:, t.n % 2 * 512:(t.n % 2 + 1) * 512] if early(t) else frt_b[:]

        def key_bank(t):
            return qry_b if early(t) else frt_b

        def quads_over(n):
            return min(max((n + L_TOK) // QUAD, 0), SLOTS // QUAD)

        def parts_out(n):
            g, at = (n + L_WC) // PER_GROUP, (n + L_WC) % PER_GROUP
            done = sum(1 + (plan[2] != 0) for p, plan in WC_PLAN.items() if p <= at)
            return min(max(PARTS_OUT * g + done, 0), PARTS_OUT * GROUPS)

        def part_of(t):
            g, at = (t.n + L_WC) // PER_GROUP, (t.n + L_WC) % PER_GROUP
            if at not in WC_PLAN or (t.static and not 0 <= g < GROUPS):
                return g, 0, None
            return g, sum(p < at for p in WC_PLAN), WC_PLAN[at]

        FOLDS = KT

        def folds(n):
            g, at = (n + L_WC) // PER_GROUP, (n + L_WC) % PER_GROUP
            if not 0 < g < GROUPS or WC_PLAN.get(at, (0, 0, 1))[2] != 0:
                return 0
            return FOLDS * (g - 1) + sum(c == 0 for p, (_, _, c) in WC_PLAN.items() if p <= at)

        def run(eng, turn):
            for n in range(FIRST_TURN, LOOP_FROM):
                turn(Turn(0, n))
            with eng.Fori(0, LOOP_COUNT) as it:
                for n in range(LOOP_FROM, LOOP_FROM + LOOP_TURNS):
                    turn(Turn(it, n))
            for n in range(LOOP_TO, LAST_TURN + 1):
                turn(Turn(0, n))

        def planes(ap):
            return ap.rearrange("p (j n i) -> p j n i", n=BLOCKS, i=BLK)

        @block.sync
        def _(sp):
            def load_group(g):
                sp.dma_start(w1g[:], ffn_w1[g]).then_inc(group_in, 16)
                sp.dma_start(w2g[:], ffn_w2[g]).then_inc(group_in, 16)
                sp.dma_start(b2g[:], ffn_b2[g]).then_inc(group_in, 16)

            def turn(t):
                q = t.quad(L_XT)
                if q is not None:
                    t.wait(sp, tok_ready, L_XT - QUAD - 1)
                    sp.dma_start(xt_in[:, q % 2], x_cols[4 * t.it + q]).then_inc(xt_loaded[q % 2], 16)
                if t.n == FIRST_TURN:
                    sp.dma_start(tw1[:], tok_w1).then_inc(scorer_in, 16)
                    sp.dma_start(tb1[:], tok_b1).then_inc(scorer_in, 16)
                    sp.dma_start(tw2[:], tok_w2).then_inc(scorer_in, 16)
                    sp.dma_start(tb2[:], tok_b2.broadcast_to([P, 1])).then_inc(scorer_in, 16)
                if t.n == -L_XW - QUAD + 1:
                    sp.dma_start(wk_s[:], w_k).then_inc(attn_in, 16)
                    sp.dma_start(wq_s[:], w_q).then_inc(attn_in, 16)
                    sp.dma_start(wv_s[:], w_v).then_inc(attn_in, 16)
                if t.n == -L_KEY - QUAD:
                    load_group(0)
                q = t.quad(L_XW + QUAD)
                if q is not None:
                    t.wait(sp, xw_ready, L_XW - 1)
                    sp.dma_start(x_in[:, q % 2], x_rows[4 * t.it + q]).then_inc(x_loaded[q % 2], 16)
                if t.n % PER_GROUP == 3 and 0 <= t.n // PER_GROUP < GROUPS - 1:
                    g = t.n // PER_GROUP + 1
                    sp.wait_ge(part_ready, PARTS_OUT * (t.it + g))
                    load_group(t.it + g)
                if t.has(L_FFN):
                    s = t.slot(L_FFN)
                    t.wait(sp, biased, L_FFN)
                    sp.dma_start(out[16 * t.it + s], h2[:, s % 8]).then_inc(stored[s % 4], 16)

            run(sp, turn)
            for i in range(4):
                sp.wait_ge(stored[i], 16 * SLOTS // 4)

        @block.gpsimd
        def _(gp):
            nc.gpsimd.memset(ident[:], 0.0).then_inc(ident_ok, 1)
            gp.wait_ge(ident_ok, 1)
            nc.gpsimd.affine_select(out=ident[:], in_=ident[:], compare_op=ALU.not_equal, fill=1.0, base=0,
                                    pattern=[[-1, P]], channel_multiplier=1).then_inc(ident_ok, 1)
            nc.gpsimd.memset(eul[:], 2.718281828459045).then_inc(ident_ok, 1)
            nc.gpsimd.memset(mone[:], -1.0).then_inc(ident_ok, 1)
            nc.gpsimd.memset(mhalf[:], -0.5).then_inc(ident_ok, 1)
            gp.wait_ge(ident_ok, 5)

            def layer_norm(t, q, lead, stat_ok, used, step, ve, dev_sq, nmean, rstd, shift):
                t.wait(gp, stat_ok, lead + QUAD - 1)
                t.wait(gp, used, lead - QUAD - 1)
                gp.sem_inc(gp_past, 1)
                b = q % 2
                nc.gpsimd.tensor_scalar(ve[:], dev_sq[:, b], 1.0 / DIM, LN_EPS, ALU.mult, ALU.add).then_inc(step, 1)
                t.wait_quad(gp, step, q, 3, 1)
                nc.gpsimd.tensor_tensor(rstd[:, b], ve[:], mhalf[:], ALU.pow).then_inc(step, 1)
                t.wait_quad(gp, step, q, 3, 2)
                nc.gpsimd.tensor_tensor(shift[:, b], nmean[:, b], rstd[:, b], ALU.mult).then_inc(step, 1)

            def square_sums(t, q):
                t.wait(gp, ksq_ready, L_SUM + QUAD - 1)
                sq = key_sq[:, (q % 2) * QUAD:(q % 2 + 1) * QUAD]
                for i, width in enumerate((DIM // 2, DIM // 4)):
                    nc.gpsimd.tensor_tensor(sq[:, :, 0:width], sq[:, :, 0:width], sq[:, :, width:2 * width],
                                            ALU.add).then_inc(sumsq_ok, 1)
                    t.wait_quad(gp, sumsq_ok, q, 3, i + 1)
                nc.gpsimd.tensor_tensor(sumsq[:, q % 2].rearrange("p (s n) -> p s n", n=BLOCKS), sq[:, :, 0:BLOCKS],
                                        sq[:, :, BLOCKS:2 * BLOCKS], ALU.add).then_inc(sumsq_ok, 1)

            def softmax(t, q):
                t.wait_quad(gp, e_ready, q, 1, 1)
                t.wait(gp, xw_ready, L_SOFT - QUAD - 1)
                b = q % 2
                nc.gpsimd.tensor_tensor(sm[:, 0], energy[:, b], energy[:, b], ALU.subtract).then_inc(sm_step, 1)
                t.wait_quad(gp, sm_step, q, 4, 1)
                nc.gpsimd.tensor_tensor(sm[:, 1], eul[:], sm[:, 0], ALU.pow).then_inc(sm_step, 1)
                t.wait_quad(gp, sm_step, q, 4, 2)
                nc.gpsimd.tensor_tensor(sm[:, 2], sm[:, 1], mone[:], ALU.pow).then_inc(sm_step, 1)
                t.wait_quad(gp, sm_step, q, 4, 3)
                nc.gpsimd.tensor_tensor(weight[:, b], sm[:, 1], sm[:, 2], ALU.mult).then_inc(sm_step, 1)

            def key_norm(t, q):
                b = q % 2
                s = sumsq[:, b]
                k = [0]

                tt, ts = nc.gpsimd.tensor_tensor, nc.gpsimd.tensor_scalar

                def step(op, dst, *args):
                    if op is ts:
                        gp.sem_inc(gp_past, 1)
                    op(dst, *args).then_inc(newt, 1)
                    k[0] += 1
                    if k[0] < NEWT:
                        t.wait_quad(gp, newt, q, NEWT, k[0])

                t.wait_quad(gp, seed_ok, q, 2, 2)
                t.wait_quad(gp, nrec_ok, q - 1, 1, 1)
                step(tt, nt[:, 1], nt[:, 2], s, ALU.mult)
                step(ts, nt[:, 2], nt[:, 1], 0.375, -1.25, ALU.mult, ALU.add)
                step(tt, nt[:, 3], nt[:, 2], nt[:, 1], ALU.mult)
                step(ts, nt[:, 2], nt[:, 3], 1.0, 1.875, ALU.mult, ALU.add)
                step(tt, root[:, 1], root[:, 0], nt[:, 2], ALU.mult)
                step(tt, nt[:, 1], root[:, 1], s, ALU.mult)
                step(tt, nt[:, 2], nt[:, 1], root[:, 1], ALU.mult)
                step(ts, nt[:, 3], nt[:, 2], 0.5, -1.5, ALU.mult, ALU.add)
                step(tt, nt[:, 0], nt[:, 3], nt[:, 1], ALU.mult)
                assert k[0] == NEWT

            def turn(t):
                if t.has(L_RET):
                    m = t.slot(L_RET)
                    q = m // QUAD
                    t.wait_quad(gp, nrec_ok, q, 1, 1)
                    t.wait(gp, key_ready, L_RET)
                    t.wait(gp, outer_done, L_RET - 4)
                    nc.gpsimd.tensor_tensor(
                        nkey[:, m % 4].rearrange("p (j n) -> p j n", n=BLOCKS),
                        key[:, m % 8].rearrange("p (j n) -> p j n", n=BLOCKS),
                        nrecip[:, q % 2, (m % QUAD) * BLOCKS:(m % QUAD + 1) * BLOCKS].unsqueeze(1)
                        .broadcast_to([P, BLK, BLOCKS]), ALU.mult).then_inc(nkey_ok, 1)
                if t.has(L_RET) and not first_step(t, L_RET):
                    t.wait(gp, nkey_ok, L_RET)
                    t.wait(gp, dT_ready, L_RET - 1)
                    for half in range(2):
                        t.wait(gp, state_new, L_RET - LANES, per=2, part=half + 1)
                        lo = half * HALF
                        nk = nkey[:, m % 4, half * P:(half + 1) * P]
                        nc.gpsimd.tensor_tensor(
                            ret_prod[:, lo:lo + HALF].rearrange("p (c i) -> p c i", i=BLK),
                            state[:, m % LANES, lo:lo + HALF].rearrange("p (c i) -> p c i", i=BLK),
                            nk.unsqueeze(2).broadcast_to([P, P, BLK]), ALU.mult).then_inc(ret_done, 1)
                if t.has(L_FFN):
                    s = t.slot(L_FFN)
                    if s % PER_GROUP == 0:
                        gp.wait_ge(bc_ready, t.it + s // PER_GROUP + 1)
                    t.wait(gp, y_ready, L_FFN)
                    nc.gpsimd.tensor_tensor(h2[:, s % 8], h2[:, s % 8], bc[:], ALU.add).then_inc(biased, 1)
                q = t.quad(L_NORM)
                if q is not None:
                    key_norm(t, q)
                q = t.quad(L_SOFT)
                if q is not None:
                    softmax(t, q)
                q = t.quad(L_LN1)
                if q is not None:
                    layer_norm(t, q, L_LN1, stat1_ok, xn_ready, ln1_step, ve1, dev_sq1, nmean1, rstd1, shift1)
                q = t.quad(L_LN2)
                if q is not None:
                    layer_norm(t, q, L_LN2, stat2_ok, xn2_ready, ln2_step, ve2, dev_sq2, nmean2, rstd2, shift2)
                q = t.quad(L_SUM)
                if q is not None:
                    square_sums(t, q)

            run(gp, turn)

        @block.tensor
        def _(pe):
            mm = nc.tensor.matmul

            def tr(dst, src, start=False, stop=False):
                return mm(dst, src, ident[:], start=start, stop=stop, is_transpose=True, skip_group_check=True)

            def plane_sums(prod, dst, done, t, lead, start, from_slot=0, count=BLK):
                for j in range(count):
                    if j % (BLK // 2) == 0:
                        t.wait(pe, done, lead, per=2, part=j // (BLK // 2) + 1, start=from_slot)
                    for h in range(KT):
                        col = j * PLANE + h * P
                        last = tr(dst[:, h * P:(h + 1) * P], prod[:, col:col + P],
                                  start=start and j == 0 and h == 0, stop=(j == count - 1))
                return last

            def scorer_read(t, back):
                t.wait(pe, th_ready, L_TOK - back)
                if not t.has(L_TOK - back):
                    pe.wait_ge(e_ready, quads_over(t.n - back))
                    pe.wait_ge(part_ready, parts_out(t.n - back))

            def product(t, g, part, h, c):
                bank = scorer_bank(t)
                if part == 0:
                    pe.wait_ge(group_in, 16 * GROUP_DMAS * (t.it + g + 1))
                for o in range(OT):
                    last = mm(bank[:, DIM:DIM + P + c], w2g[:, o, h * P:(h + 1) * P],
                              w1g[:, o, c * P:(c + 1) * P + c], start=(o == 0), stop=(o == OT - 1),
                              skip_group_check=True)
                last.then_inc(part_b_ready, 1)

            def turn(t):
                if t.has(L_OUT):
                    t.wait(pe, dT_out, L_DEL - 1)
                    number = folds(t.n - 1)
                    if number:
                        pe.wait_ge(folded, FOLDS * t.it + number)
                    plane_sums(out_prod, rec_b, outp_done, t, L_OUT, start=True,
                               count=BLK // 2 if number else BLK).then_inc(sqT_ready, 1)
                if t.has(L_KEY) or t.has(L_FFN):
                    if early(t):
                        t.wait(pe, xnT_ready, L_KEY - 1)
                    else:
                        t.wait(pe, ksq_ready, L_KEY - 1)
                    if not t.has(L_KEY - 1):
                        t.wait(pe, xn2T_ready, L_FFN - 1)
                        scorer_read(t, 1)
                    if t.has(L_KEY):
                        s = t.slot(L_KEY)
                        t.wait(pe, xn_ready, L_KEY)
                        for k in range(KT):
                            last = tr(frt_b[:, k * P:(k + 1) * P], xn[:, s % 2, k * P:(k + 1) * P],
                                      start=(k == 0), stop=True)
                    if t.has(L_FFN):
                        s = t.slot(L_FFN)
                        t.wait(pe, xn2_ready, L_FFN)
                        for k in range(KT):
                            last = tr(frt_b[:, DIM + k * P:DIM + (k + 1) * P], xn2[:, s % 2, k * P:(k + 1) * P],
                                      start=(k == 0 and not t.has(L_KEY)), stop=True)
                    last.then_inc(tr_ready, 1)
                if t.has(L_QRY):
                    s = t.slot(L_QRY)
                    t.wait(pe, outp_done, L_QRY - 1, per=2)
                    for k in range(KT):
                        last = mm(qry_b[:, 0:DIM], xnT[:, s % 16, k, :], wq_s[:, k, :], start=(k == 0),
                                  stop=(k == KT - 1))
                    last.then_inc(qry_ready, 1)
                g, part, plan = part_of(t)
                product_first = bool(folds(t.n - 1))
                if product_first:
                    t.wait(pe, xnT_ready, L_KEY)
                    t.wait(pe, xn2T_ready, L_FFN)
                    product(t, g, part, *plan[1:])
                if t.has(L_OUT) or t.has(L_FFN):
                    t.wait(pe, outer_done, L_UPD)
                    if t.has(L_OUT):
                        s = t.slot(L_OUT)
                        t.wait(pe, outT_ready, L_OUT)
                        for h in range(KT):
                            last = tr(del_b[:, h * P:(h + 1) * P], outT[:, s % 2, h, :], start=(h == 0), stop=True)
                    if t.has(L_FFN):
                        s = t.slot(L_FFN)
                        if not t.has(L_DEL - 1):
                            t.wait(pe, h2_ready, L_OUT - 1)
                            t.wait(pe, y_ready, L_FFN - 1)
                        t.wait(pe, xn2T_ready, L_FFN)
                        if s % PER_GROUP == 0:
                            pe.wait_ge(wc_ready, t.it + s // PER_GROUP + 1)
                        for k in range(KT):
                            last = mm(del_b[:, DIM:2 * DIM], xn2T[:, s % 2, k, :], wc[:, k, :],
                                      start=(k == 0 and not t.has(L_OUT)), stop=(k == KT - 1), skip_group_check=True)
                    last.then_inc(ik_ready, 1)
                q = t.n + L_TOK - QUAD
                quad_over = q % QUAD == 0 and t.has(L_TOK - QUAD)
                opened = False
                if quad_over or t.has(L_TOK) or plan:
                    if t.n == -L_TOK:
                        pe.wait_ge(scorer_in, 16 * SCORER_DMAS)
                        pe.wait_ge(ident_ok, 2)
                    if early(t):
                        scorer_read(t, 2)
                    else:
                        t.wait(pe, xnT_ready, L_KEY)
                        t.wait(pe, xn2T_ready, L_FFN)
                bank = scorer_bank(t)
                if plan:
                    kind, h, c = plan
                    if kind == "product":
                        if not product_first:
                            product(t, g, part, h, c)
                    else:
                        assert not quad_over
                        pe.wait_ge(part_ready, PARTS_OUT * (t.it + g) + (h + 1) * PARTS_OUT // KT - 2)
                        for k in range(KT):
                            tr(bank[:, DIM + k * P:DIM + (k + 1) * P], wcT_half[:, k * P:(k + 1) * P],
                               start=(k == 0), stop=True)
                        last = tr(bank[:, P:2 * P], bc_col[:, h:h + 1].broadcast_to([P, P]), stop=True)
                        last.then_inc(part_b_ready, 1)
                    opened = True
                if quad_over:
                    pe.wait_ge(th_ready, 16 * t.it + q + QUAD)
                    for i in range(QUAD):
                        last = mm(bank[:, P + i:P + i + 1], th[:, i, :], tw2[:],
                                  start=(i == 0 and not opened), stop=True, skip_group_check=True)
                    opened = True
                    last.then_inc(en_ready, 1)
                if t.has(L_TOK):
                    s = t.slot(L_TOK)
                    if s % QUAD == 0:
                        pe.wait_ge(xt_loaded[s // QUAD % 2], 32 * t.it + 16 * (s // QUAD // 2 + 1))
                    for k in range(KT):
                        last = mm(bank[:, 0:P], tw1[:, k, :], xt_in[:, s // QUAD % 2, s % QUAD, k, :],
                                  start=(k == 0 and not opened), stop=(k == KT - 1), skip_group_check=True)
                    last.then_inc(tok_ready, 1)
                if t.has(L_DEL):
                    s = t.slot(L_DEL)
                    t.wait(pe, outT_ready, L_OUT)
                    for h in range(KT):
                        for k in range(KT):
                            last = mm(rec_b[:, h * P:(h + 1) * P], wv_s[:, k, h * P:(h + 1) * P],
                                      xnT[:, s % 16, k, :], start=(h == 0 and k == 0),
                                      stop=(first_step(t, L_DEL) and k == KT - 1), skip_group_check=True)
                    if not first_step(t, L_DEL):
                        last = plane_sums(ret_prod, rec_b, ret_done, t, L_DEL, start=False, from_slot=LANES)
                    last.then_inc(dT_ready, 1)
                if t.has(L_KEY):
                    s = t.slot(L_KEY)
                    t.wait(pe, xnT_ready, L_KEY)
                    t.wait(pe, xn2T_ready, L_FFN)
                    if s == 0:
                        pe.wait_ge(attn_in, 16 * ATTN_DMAS)
                    if early(t):
                        t.wait(pe, ksq_ready, L_KEY - 1)
                    else:
                        scorer_read(t, 0)
                    for k in range(KT):
                        last = mm(key_bank(t)[:, 0:DIM], xnT[:, s % 16, k, :], wk_s[:, k, :], start=(k == 0),
                                  stop=(k == KT - 1))
                    last.then_inc(key_b_ready, 1)
                if t.has(L_DEL):
                    s = t.slot(L_DEL)
                    t.wait(pe, dT_out, L_DEL)
                    t.wait(pe, outer_done, L_DEL - 1)
                    t.wait(pe, h2_ready, L_OUT)
                    t.wait(pe, y_ready, L_FFN)
                    for h in range(KT):
                        last = tr(del_b[:, h * P:(h + 1) * P], deltaT[:, s % 2, h, :], start=(h == 0), stop=True)
                    last.then_inc(del_ready, 1)

            run(pe, turn)

        @block.scalar
        def _(act):
            fn = nc.scalar.activation
            act.wait_ge(ident_ok, 2)
            fn(warm[:], ident[:, 0:1], ACT.Silu).then_inc(warm_ok, 1)

            def normalise(t):
                if t.has(L_KEY):
                    s = t.slot(L_KEY)
                    qp = s // QUAD % 2
                    t.wait_quad(act, ln1_step, s // QUAD, 3, 3)
                    fn(xn[:, s % 2], xw[:, s % 16], ACT.Identity, scale=rstd1[:, qp, s % QUAD:s % QUAD + 1],
                       bias=shift1[:, qp, s % QUAD:s % QUAD + 1]).then_inc(xn_ready, 1)
                if t.has(L_FFN):
                    s = t.slot(L_FFN)
                    qp = s // QUAD % 2
                    t.wait_quad(act, ln2_step, s // QUAD, 3, 3)
                    fn(xn2[:, s % 2], h2[:, s % 8], ACT.Identity, scale=rstd2[:, qp, s % QUAD:s % QUAD + 1],
                       bias=shift2[:, qp, s % QUAD:s % QUAD + 1]).then_inc(xn2_ready, 1)

            def scorer(t):
                g, part, plan = part_of(t)
                q = t.n + L_TOK - QUAD
                quad_over = q % QUAD == 0 and t.has(L_TOK - QUAD)
                if plan or quad_over or t.has(L_TOK):
                    if t.n == -L_TOK:
                        act.wait_ge(scorer_in, 16 * SCORER_DMAS)
                    if plan:
                        act.wait_ge(part_b_ready, PARTS * (t.it + g) + part + 1)
                    if quad_over:
                        act.wait_ge(en_ready, 4 * t.it + q // QUAD + 1)
                    t.wait(act, tok_ready, L_TOK)
                bank = scorer_bank(t)
                if plan:
                    kind, h, c = plan
                    if part == 0 and (not t.static or g > 0):
                        act.wait_ge(wc_ready, t.it + g)
                    if kind == "product":
                        fn(wcT_half[:, c * P:(c + 1) * P], bank[:, DIM:DIM + P], ACT.Copy).then_inc(part_ready, 1)
                        if c == 1:
                            fn(bc_col[:, h:h + 1], bank[:, DIM + P:DIM + P + 1], ACT.Identity,
                               bias=b2g[:, h:h + 1]).then_inc(part_ready, 1)
                    else:
                        fn(wc_next[:, :, h * P:(h + 1) * P],
                           bank[:, DIM:2 * DIM].rearrange("p (k c) -> p k c", k=KT), ACT.Copy).then_inc(part_ready, 1)
                        if h == 0 and (not t.static or g > 0):
                            act.wait_ge(bc_ready, t.it + g)
                        fn(bc_next[:, h * P:(h + 1) * P], bank[:, P:2 * P], ACT.Copy).then_inc(part_ready, 1)
                if quad_over:
                    t.wait_quad(act, sm_step, q // QUAD - 2, 4, 4)
                    fn(energy[:, q // QUAD % 2], bank[:, P:P + QUAD], ACT.Identity, bias=tb2[:]).then_inc(e_ready, 1)
                if t.has(L_TOK):
                    s = t.slot(L_TOK)
                    fn(th[:, s % QUAD], bank[:, 0:P], ACT.Tanh, bias=tb1[:]).then_inc(th_ready, 1)

            def turn(t):
                if not early(t):
                    normalise(t)
                if t.has(L_FFN) and t.slot(L_FFN) % PER_GROUP == 0:
                    g = t.slot(L_FFN) // PER_GROUP
                    act.wait_ge(part_ready, PARTS_OUT * (t.it + g + 1))
                    t.wait(act, y_ready, L_FFN - 1)
                    fn(wc[:], wc_next[:], ACT.Copy).then_inc(wc_ready, 1)
                if t.has(L_OUT):
                    s = t.slot(L_OUT)
                    t.wait(act, sqT_ready, L_OUT)
                    fn(silu[:, s % 2], rec_b[:, 0:DIM], ACT.Silu).then_inc(silu_ready, 1)
                if t.has(L_KEY) or t.has(L_FFN):
                    act.wait_ge(tr_ready, 16 * t.it + t.n + L_KEY + 1)
                    if t.has(L_FFN):
                        s = t.slot(L_FFN)
                        fn(xn2T[:, s % 2].rearrange("p k b -> p (k b)"), frt_b[:, DIM:2 * DIM],
                           ACT.Copy).then_inc(xn2T_ready, 1)
                    if t.has(L_KEY):
                        s = t.slot(L_KEY)
                        t.wait(act, qry_ready, L_KEY - 16)
                        fn(xnT[:, s % 16].rearrange("p k b -> p (k b)"), frt_b[:, 0:DIM],
                           ACT.Copy).then_inc(xnT_ready, 1)
                if t.has(L_STAT2):
                    s = t.slot(L_STAT2)
                    qp, i = s // QUAD % 2, s % QUAD
                    if i == 0:
                        t.wait_quad(act, ln2_step, s // QUAD - 2, 3, 3)
                    t.wait(act, h2_ready, L_STAT2)
                    t.wait(act, stat1_ok, L_XW - 1)
                    t.wait(act, stat2_ok, L_STAT2 - 1)
                    fn(dev[:], h2[:, s % 8], ACT.Copy, accum_out=sum2[:, s % 2:s % 2 + 1]).then_inc(sum2_ok, 1)
                    t.wait(act, sum2_ok, L_STAT2)
                    fn(nmean2[:, qp, i:i + 1], sum2[:, s % 2:s % 2 + 1], ACT.Copy,
                       scale=-1.0 / DIM).then_inc(nmean2_ok, 1)
                    t.wait(act, nmean2_ok, L_STAT2)
                    fn(dev[:], h2[:, s % 8], ACT.Square, bias=nmean2[:, qp, i:i + 1],
                       accum_out=dev_sq2[:, qp, i:i + 1]).then_inc(stat2_ok, 1)
                for half in range(2):
                    if half == 1 and not early(t):
                        scorer(t)
                    if t.has(L_UPD):
                        s = t.slot(L_UPD)
                        lo = half * HALF
                        if first_step(t, L_UPD):
                            t.wait(act, outer_done, L_UPD)
                            fn(state[:, s % LANES, lo:lo + HALF], upd[:, lo:lo + HALF], ACT.Tanh,
                               scale=-1.0).then_inc(state_new, 1)
                        else:
                            t.wait(act, sum_done, L_UPD, per=2, part=half + 1, start=LANES)
                            fn(state[:, s % LANES, lo:lo + HALF], upd[:, lo:lo + HALF],
                               ACT.Tanh).then_inc(state_new, 1)
                if t.has(L_XW):
                    s = t.slot(L_XW)
                    qp, i = s // QUAD % 2, s % QUAD
                    if i == 0:
                        act.wait_ge(x_loaded[qp], 32 * t.it + 16 * (s // QUAD // 2 + 1))
                        t.wait_quad(act, sm_step, s // QUAD, 4, 4)
                        t.wait_quad(act, ln1_step, s // QUAD - 2, 3, 3)
                    t.wait(act, h2_ready, L_XW - 16)
                    fn(xw[:, s % 16], x_in[:, qp, i], ACT.Copy, scale=weight[:, qp, i:i + 1],
                       accum_out=sum1[:, s % 2:s % 2 + 1]).then_inc(xw_ready, 1)
                    t.wait(act, xw_ready, L_XW)
                    fn(nmean1[:, qp, i:i + 1], sum1[:, s % 2:s % 2 + 1], ACT.Copy,
                       scale=-1.0 / DIM).then_inc(nmean1_ok, 1)
                if t.has(L_DEL):
                    s = t.slot(L_DEL)
                    t.wait(act, dT_ready, L_DEL)
                    fn(deltaT[:, s % 2].rearrange("p h b -> p (h b)"), rec_b[:, 0:DIM], ACT.Copy).then_inc(dT_out, 1)
                if t.has(L_XW):
                    s = t.slot(L_XW)
                    qp, i = s // QUAD % 2, s % QUAD
                    t.wait(act, nmean1_ok, L_XW)
                    t.wait(act, stat1_ok, L_XW - 1)
                    t.wait(act, stat2_ok, L_STAT2)
                    fn(dev[:], xw[:, s % 16], ACT.Square, bias=nmean1[:, qp, i:i + 1],
                       accum_out=dev_sq1[:, qp, i:i + 1]).then_inc(stat1_ok, 1)
                if t.static and early(Turn(0, t.n + 1)):
                    normalise(Turn(0, t.n + 1))
                if early(t):
                    scorer(t)
                if t.has(L_KEY):
                    s = t.slot(L_KEY)
                    t.wait(act, key_b_ready, L_KEY)
                    t.wait(act, nkey_ok, L_KEY - 8)
                    bank = key_bank(t)
                    fn(key[:, s % 8], bank[:, 0:DIM], ACT.Copy).then_inc(key_ready, 1)
                    if s % QUAD == 0:
                        t.wait_quad(act, sumsq_ok, s // QUAD - 2, 3, 3)
                    fn(key_sq[:, s % 8], bank[:, 0:DIM], ACT.Square).then_inc(ksq_ready, 1)
                if t.has(L_FFN) and t.slot(L_FFN) % PER_GROUP == 0:
                    t.wait(act, biased, L_FFN - 1)
                    fn(bc[:], bc_next[:], ACT.Copy).then_inc(bc_ready, 1)

            run(act, turn)

        @block.vector
        def _(dve):
            tt = nc.vector.tensor_tensor

            def turn(t):
                if t.has(L_UPD):
                    s = t.slot(L_UPD)
                    t.wait(dve, nkey_ok, L_UPD)
                    t.wait(dve, del_ready, L_UPD)
                    nk = nkey[:, s % 4].rearrange("p (j n) -> p j n", n=BLOCKS)
                    delta = del_b[:, 0:DIM].rearrange("p (n i) -> p n i", i=BLK)
                    if t.static and t.n == -L_UPD:
                        t.wait(dve, th_ready, L_TOK - 1)
                    t.wait(dve, state_new, L_UPD - 1, per=2)
                    tt(planes(upd[:]), delta.unsqueeze(1).broadcast_to([P, BLK, BLOCKS, BLK]),
                       nk.unsqueeze(3).broadcast_to([P, BLK, BLOCKS, BLK]), ALU.mult).then_inc(outer_done, 1)
                if t.has(L_OUT):
                    s = t.slot(L_OUT)
                    t.wait(dve, silu_ready, L_OUT)
                    tt(outT[:, s % 2].rearrange("p h b -> p (h b)"), rec_b[:, 0:DIM], silu[:, s % 2],
                       ALU.mult).then_inc(outT_ready, 1)
                if t.has(L_UPD):
                    s = t.slot(L_UPD)
                    for half in range(0 if first_step(t, L_UPD) else 2):
                        lo = half * HALF
                        t.wait(dve, outer_done, L_UPD)
                        tt(upd[:, lo:lo + HALF], state[:, s % LANES, lo:lo + HALF], upd[:, lo:lo + HALF],
                           ALU.subtract).then_inc(sum_done, 1)
                if t.has(L_OUT) or t.has(L_FFN):
                    dve.wait_ge(ik_ready, 16 * t.it + t.n + L_OUT + 1)
                if t.has(L_OUT):
                    s = t.slot(L_OUT)
                    t.wait_quad(dve, stored[s % 4], (s - 8) // 4, 16, 16)
                    tt(h2[:, s % 8], del_b[:, 0:DIM], xw[:, s % 16], ALU.add).then_inc(h2_ready, 1)
                if t.has(L_FFN):
                    s = t.slot(L_FFN)
                    tt(h2[:, s % 8], del_b[:, DIM:2 * DIM], h2[:, s % 8], ALU.add).then_inc(y_ready, 1)
                if t.has(L_QRY):
                    s = t.slot(L_QRY)
                    t.wait(dve, qry_ready, L_QRY)
                    t.wait(dve, sqT_ready, L_QRY - 1)
                    for half in range(2):
                        lo = half * HALF
                        t.wait(dve, state_new, L_QRY, per=2, part=half + 1)
                        tt(out_prod[:, lo:lo + HALF].rearrange("p (c i) -> p c i", i=BLK),
                           state[:, s % LANES, lo:lo + HALF].rearrange("p (c i) -> p c i", i=BLK),
                           qry_b[:, half * P:(half + 1) * P].unsqueeze(2).broadcast_to([P, P, BLK]),
                           ALU.mult).then_inc(outp_done, 1)
                    number = folds(t.n)
                    if number:
                        t.wait(dve, outp_done, L_QRY, per=2)
                        tt(out_prod[:, 0:HALF], out_prod[:, 0:HALF], out_prod[:, HALF:STATE],
                           ALU.add).then_inc(folded, 1)
                q = t.quad(L_INV)
                if q is not None:
                    t.wait_quad(dve, newt, q, NEWT, NEWT)
                    t.wait(dve, nkey_ok, L_INV - QUAD - 1)
                    nc.vector.tensor_scalar(nnorm[:], nt[:, 0], 1.0, -NORM_EPS, ALU.mult, ALU.add).then_inc(nnorm_ok, 1)
                    t.wait_quad(dve, nnorm_ok, q, 1, 1)
                    nc.vector.reciprocal(nrecip[:, q % 2], nnorm[:]).then_inc(nrec_ok, 1)
                q = t.quad(L_SEED)
                if q is not None:
                    t.wait_quad(dve, sumsq_ok, q, 3, 3)
                    t.wait_quad(dve, newt, q - 1, NEWT, NEWT)
                    nc.vector.tensor_scalar(nt[:, 3].bitcast(i32), sumsq[:, q % 2].bitcast(i32), 1, None,
                                            ALU.logical_shift_right).then_inc(seed_sh, 1)
                    t.wait_quad(dve, seed_sh, q, 1, 1)
                    nc.vector.tensor_scalar(root[:, 0].bitcast(i32), nt[:, 3].bitcast(i32), -1.0, float(0x5f3759df),
                                            ALU.mult, ALU.add).then_inc(seed_ok, 1)
                    t.wait_quad(dve, seed_ok, q, 2, 1)
                    tt(nt[:, 2], root[:, 0], root[:, 0], ALU.mult).then_inc(seed_ok, 1)

            run(dve, turn)


def kernel(x, L0_tok_W1, L0_tok_b1, L0_tok_W2, L0_tok_b2, L0_attn_W_k, L0_attn_W_v, L0_attn_W_q,
           L0_ffn_W1, L0_ffn_b1, L0_ffn_W2, L0_ffn_b2):
    import numpy as np
    import concourse.bacc as bacc
    from concourse import mybir
    from concourse.bass_utils import run_bass_kernel_spmd

    rows = np.asarray(x).reshape(SLOTS, P, DIM)
    x_rows = rows.reshape(SLOTS // QUAD, QUAD, P, DIM).transpose(0, 2, 1, 3)
    x_cols = rows.reshape(SLOTS // QUAD, QUAD, P, KT, P).transpose(0, 4, 1, 3, 2)

    def jn(w):
        return np.asarray(w).reshape(BLOCKS, BLK, KT, P).transpose(3, 2, 1, 0).reshape(P, KT, DIM)

    arrays = {
        "x_rows": x_rows,
        "x_cols": x_cols,
        "tok_w1": np.asarray(L0_tok_W1).reshape(KT, P, HIDDEN).transpose(1, 0, 2),
        "tok_b1": np.asarray(L0_tok_b1).reshape(P, 1),
        "tok_w2": np.asarray(L0_tok_W2),
        "tok_b2": np.asarray(L0_tok_b2).reshape(1, 1),
        "w_k": jn(L0_attn_W_k),
        "w_q": jn(L0_attn_W_q),
        "w_v": np.asarray(L0_attn_W_v).reshape(DIM, KT, P).transpose(2, 1, 0),
        "ffn_w1": np.concatenate([np.asarray(L0_ffn_W1).reshape(GROUPS, P, OT, DIM),
                                  np.asarray(L0_ffn_b1).reshape(GROUPS, P, OT, 1)], axis=3),
        "ffn_w2": np.asarray(L0_ffn_W2).transpose(0, 2, 1).reshape(GROUPS, P, OT, DIM),
        "ffn_b2": np.asarray(L0_ffn_b2).reshape(GROUPS, KT, P).transpose(0, 2, 1),
    }
    arrays = {name: np.ascontiguousarray(a) for name, a in arrays.items()}
    nc = bacc.Bacc("TRN2", target_bir_lowering=False, num_devices=1)
    args = [nc.dram_tensor(name, a.shape, mybir.dt.float32, kind="ExternalInput").ap() for name, a in arrays.items()]
    out = nc.dram_tensor("out", (SLOTS, P, DIM), mybir.dt.float32, kind="ExternalOutput").ap()
    by_name = dict(zip(arrays, args))
    vit_tower_kernel(nc, out=out, **by_name)
    r = run_bass_kernel_spmd(nc, [arrays], core_ids=[0])
    return r.results[0]["out"].reshape(STEPS, BATCH, DIM)
```
